# Optimizing a Trainium2 kernel written in Bass

```python
import numpy as np
import jax
import jax.numpy as jnp

def _softmax(x, axis=-1):
    return jax.nn.softmax(x, axis=axis)

def _gelu(x):
    return jax.nn.gelu(x, approximate=True)

def _silu(x):
    return jax.nn.silu(x)

def _sigmoid(x):
    return jax.nn.sigmoid(x)

def _layernorm(x, axis=-1, eps=1e-05):
    m = jnp.mean(x, axis=axis, keepdims=True)
    v = jnp.var(x, axis=axis, keepdims=True)
    return (x - m) / jnp.sqrt(v + eps)

def _scatter_add(tgt, idx, src, axis=0):
    return tgt.at[idx].add(src)

def _segment_sum(src, seg, n):
    return jax.ops.segment_sum(src, seg, n)
kernel_name = 'mk_decoder_preln_d1_seqx_r8_e6a80b'

def setup_inputs(seed: int=0):
    np.random.seed(seed)
    _w = jnp.asarray

    def _rec_inputs():
        import jax
        import jax.numpy as jnp
        _rk = jax.random.key(seed)
        x = 0.000341 + 1 * jax.random.normal(jax.random.fold_in(_rk, 1), (8, 128, 256), jnp.float32)
        _lenS = 128 - jax.random.randint(jax.random.fold_in(_rk, 7), (8,), 0, max(1, 128 // 4) + 1, jnp.int32)
        _lenS2 = 128 - jax.random.randint(jax.random.fold_in(_rk, 8), (8,), 0, max(1, 128 // 4) + 1, jnp.int32)
        _ctx_2048P = jax.random.normal(jax.random.fold_in(_rk, 11), (8, 16, 256), jnp.float32)
        _ctx_2048c = jax.random.dirichlet(jax.random.fold_in(_rk, 511), 0.3 * jnp.ones((16,), jnp.float32), (8, 128))
        _ctx_2048t = jnp.einsum('bsk,bkd->bsd', _ctx_2048c, _ctx_2048P)
        _ctx_2048t = _ctx_2048t * jax.lax.rsqrt(jnp.mean(jnp.square(_ctx_2048t)) + 1e-12) * 0.953939
        ctx_2048 = -1.47943e-05 + 1.00017 * (_ctx_2048t + 0.3 * jax.random.normal(jax.random.fold_in(_rk, 611), (8, 128, 256), jnp.float32))
        return (x, ctx_2048)
    x, ctx_2048 = _rec_inputs()

    def _L0_attn_setup():
        import jax, jax.numpy as jnp
        import numpy as np
        BLOCK = 32
        NUM_HEADS = 16
        HEAD_DIM = 128
        FP4_GRID = jnp.array([0.0, 0.5, 1.0, 1.5, 2.0, 3.0, 4.0, 6.0], dtype=jnp.float32)

        def quantize_to_mxfp4(w, block_size=BLOCK):
            D, F = w.shape
            blocks = w.reshape(D // block_size, block_size, F)
            amax = jnp.max(jnp.abs(blocks), axis=1)
            e = jnp.floor(jnp.log2(jnp.maximum(amax, 1e-12) / 6.0))
            scale = jnp.exp2(e)
            v = blocks / scale[:, None, :]
            idx = jnp.argmin(jnp.abs(jnp.abs(v)[..., None] - FP4_GRID), axis=-1)
            codes = jnp.sign(v) * FP4_GRID[idx]
            return (codes.reshape(D, F).astype(jnp.float32), scale.astype(jnp.float32))

        def _mxfp4_matmul(x, codes, scales, block_size=BLOCK):
            w = codes * jnp.repeat(scales, block_size, axis=0)
            return x @ w
        key = jax.random.key(seed)
        ks = jax.random.split(key, 9)
        B, S, D = (2, 256, 256)
        feat = NUM_HEADS * HEAD_DIM
        x = jax.random.normal(ks[0], (B, S, D), dtype=jnp.float32)

        def make_w(k, din, dout):
            w = jax.random.normal(k, (din, dout), dtype=jnp.float32) * (1.0 / np.sqrt(din))
            return quantize_to_mxfp4(w, BLOCK)
        wq_codes, wq_scales = make_w(ks[1], D, feat)
        wk_codes, wk_scales = make_w(ks[2], D, feat)
        wv_codes, wv_scales = make_w(ks[3], D, feat)
        wo_codes, wo_scales = make_w(ks[4], feat, D)
        bq = jnp.zeros((feat,), jnp.float32)
        bk = jnp.zeros((feat,), jnp.float32)
        bv = jnp.zeros((feat,), jnp.float32)
        bo = jnp.zeros((D,), jnp.float32)
        return {'x': x, 'wq_codes': wq_codes, 'wq_scales': wq_scales, 'bq': bq, 'wk_codes': wk_codes, 'wk_scales': wk_scales, 'bk': bk, 'wv_codes': wv_codes, 'wv_scales': wv_scales, 'bv': bv, 'wo_codes': wo_codes, 'wo_scales': wo_scales, 'bo': bo}
    _L0_attn_all = _L0_attn_setup()
    _L0_attn_in = {k: v for k, v in _L0_attn_all.items() if k in ('wq_codes', 'wq_scales', 'bq', 'wk_codes', 'wk_scales', 'bk', 'wv_codes', 'wv_scales', 'bv', 'wo_codes', 'wo_scales', 'bo')}
    del _L0_attn_all

    def _L0_xattn_setup():
        import jax, jax.numpy as jnp
        import numpy as np

        def _wkv(time_decay, time_first, k, v):
            w = -jnp.exp(time_decay)
            u = time_first
            B, T, C = k.shape
            aa = jnp.zeros((B, C), dtype=k.dtype)
            bb = jnp.zeros((B, C), dtype=k.dtype)
            pp = jnp.full((B, C), -1e+38, dtype=k.dtype)

            def step(carry, kv_t):
                aa, bb, pp = carry
                kt, vt = kv_t
                ww = u + kt
                q = jnp.maximum(pp, ww)
                e1 = jnp.exp(pp - q)
                e2 = jnp.exp(ww - q)
                y_t = (e1 * aa + e2 * vt) / (e1 * bb + e2)
                ww2 = pp + w
                q2 = jnp.maximum(ww2, kt)
                e1b = jnp.exp(ww2 - q2)
                e2b = jnp.exp(kt - q2)
                new_carry = (e1b * aa + e2b * vt, e1b * bb + e2b, q2)
                return (new_carry, y_t)
            ks = jnp.transpose(k, (1, 0, 2))
            vs = jnp.transpose(v, (1, 0, 2))
            _, ys = jax.lax.scan(step, (aa, bb, pp), (ks, vs))
            return jnp.transpose(ys, (1, 0, 2))
        key = jax.random.key(seed)
        k1, k2, k3, k4 = jax.random.split(key, 4)
        B, T, C = (8, 128, 256)
        return {'batch_size': B, 'seq_len': T, 'embedding_dim': C, 'time_decay': jax.random.normal(k1, (C,), dtype=jnp.float32), 'time_first': jax.random.normal(k2, (C,), dtype=jnp.float32), 'k': jax.random.normal(k3, (B, T, C), dtype=jnp.float32), 'v': jax.random.normal(k4, (B, T, C), dtype=jnp.float32)}
    _L0_xattn_all = _L0_xattn_setup()
    _L0_xattn_in = {k: v for k, v in _L0_xattn_all.items() if k in ('time_decay', 'time_first')}
    del _L0_xattn_all

    def _L0_ffn_setup():
        import jax, jax.numpy as jnp
        import numpy as np
        NUM_ROUTED = 7
        TOP_K = 3
        D = 256
        H = 256
        B, S = (4, 256)

        def _expert_ffn(x, w1, wg, w2):
            return jax.nn.silu(x @ w1) * (x @ wg) @ w2
        key = jax.random.key(seed)
        ks = jax.random.split(key, 8)
        s = 0.02
        return {'x': jax.random.normal(ks[0], (B, S, D), jnp.float32), 'W1': jax.random.normal(ks[1], (NUM_ROUTED, D, H), jnp.float32) * s, 'Wg': jax.random.normal(ks[2], (NUM_ROUTED, D, H), jnp.float32) * s, 'W2': jax.random.normal(ks[3], (NUM_ROUTED, H, D), jnp.float32) * s, 'Ws1': jax.random.normal(ks[4], (D, H), jnp.float32) * s, 'Wsg': jax.random.normal(ks[5], (D, H), jnp.float32) * s, 'Ws2': jax.random.normal(ks[6], (H, D), jnp.float32) * s, 'gate_w': jax.random.normal(ks[7], (D, NUM_ROUTED), jnp.float32) * s, 'gate_b': jnp.zeros((NUM_ROUTED,), jnp.float32), 'biases': jnp.zeros((NUM_ROUTED,), jnp.float32)}
    _L0_ffn_all = _L0_ffn_setup()
    _L0_ffn_in = {k: v for k, v in _L0_ffn_all.items() if k in ('W1', 'Wg', 'W2', 'Ws1', 'Wsg', 'Ws2', 'gate_w', 'gate_b', 'biases')}
    del _L0_ffn_all
    return {'x': x, 'ctx_2048': ctx_2048, 'L0_attn_wq_codes': _L0_attn_in['wq_codes'], 'L0_attn_wq_scales': _L0_attn_in['wq_scales'], 'L0_attn_bq': _L0_attn_in['bq'], 'L0_attn_wk_codes': _L0_attn_in['wk_codes'], 'L0_attn_wk_scales': _L0_attn_in['wk_scales'], 'L0_attn_bk': _L0_attn_in['bk'], 'L0_attn_wv_codes': _L0_attn_in['wv_codes'], 'L0_attn_wv_scales': _L0_attn_in['wv_scales'], 'L0_attn_bv': _L0_attn_in['bv'], 'L0_attn_wo_codes': _L0_attn_in['wo_codes'], 'L0_attn_wo_scales': _L0_attn_in['wo_scales'], 'L0_attn_bo': _L0_attn_in['bo'], 'L0_xattn_time_decay': _L0_xattn_in['time_decay'], 'L0_xattn_time_first': _L0_xattn_in['time_first'], 'L0_ffn_W1': _L0_ffn_in['W1'], 'L0_ffn_Wg': _L0_ffn_in['Wg'], 'L0_ffn_W2': _L0_ffn_in['W2'], 'L0_ffn_Ws1': _L0_ffn_in['Ws1'], 'L0_ffn_Wsg': _L0_ffn_in['Wsg'], 'L0_ffn_Ws2': _L0_ffn_in['Ws2'], 'L0_ffn_gate_w': _L0_ffn_in['gate_w'], 'L0_ffn_gate_b': _L0_ffn_in['gate_b'], 'L0_ffn_biases': _L0_ffn_in['biases']}

def reference(x, ctx_2048, L0_attn_wq_codes, L0_attn_wq_scales, L0_attn_bq, L0_attn_wk_codes, L0_attn_wk_scales, L0_attn_bk, L0_attn_wv_codes, L0_attn_wv_scales, L0_attn_bv, L0_attn_wo_codes, L0_attn_wo_scales, L0_attn_bo, L0_xattn_time_decay, L0_xattn_time_first, L0_ffn_W1, L0_ffn_Wg, L0_ffn_W2, L0_ffn_Ws1, L0_ffn_Wsg, L0_ffn_Ws2, L0_ffn_gate_w, L0_ffn_gate_b, L0_ffn_biases):
    import jax
    import jax.numpy as jnp

    def _L0_attn_ref(x, wq_codes, wq_scales, bq, wk_codes, wk_scales, bk, wv_codes, wv_scales, bv, wo_codes, wo_scales, bo):
        import jax, jax.numpy as jnp
        import numpy as np
        BLOCK = 32
        NUM_HEADS = 16
        HEAD_DIM = 128
        FP4_GRID = jnp.array([0.0, 0.5, 1.0, 1.5, 2.0, 3.0, 4.0, 6.0], dtype=jnp.float32)

        def quantize_to_mxfp4(w, block_size=BLOCK):
            D, F = w.shape
            blocks = w.reshape(D // block_size, block_size, F)
            amax = jnp.max(jnp.abs(blocks), axis=1)
            e = jnp.floor(jnp.log2(jnp.maximum(amax, 1e-12) / 6.0))
            scale = jnp.exp2(e)
            v = blocks / scale[:, None, :]
            idx = jnp.argmin(jnp.abs(jnp.abs(v)[..., None] - FP4_GRID), axis=-1)
            codes = jnp.sign(v) * FP4_GRID[idx]
            return (codes.reshape(D, F).astype(jnp.float32), scale.astype(jnp.float32))

        def _mxfp4_matmul(x, codes, scales, block_size=BLOCK):
            w = codes * jnp.repeat(scales, block_size, axis=0)
            return x @ w
        B, S, D = x.shape
        q = _mxfp4_matmul(x, wq_codes, wq_scales) + bq
        k = _mxfp4_matmul(x, wk_codes, wk_scales) + bk
        v = _mxfp4_matmul(x, wv_codes, wv_scales) + bv
        q = q.reshape(B, S, NUM_HEADS, HEAD_DIM)
        k = k.reshape(B, S, NUM_HEADS, HEAD_DIM)
        v = v.reshape(B, S, NUM_HEADS, HEAD_DIM)
        scores = jnp.einsum('bqhd,bkhd->bhqk', q, k) / jnp.sqrt(jnp.float32(HEAD_DIM))
        attn = jax.nn.softmax(scores, axis=-1)
        out = jnp.einsum('bhqk,bkhd->bqhd', attn, v).reshape(B, S, NUM_HEADS * HEAD_DIM)
        return _mxfp4_matmul(out, wo_codes, wo_scales) + bo

    def _L0_xattn_ref(batch_size, seq_len, embedding_dim, time_decay, time_first, k, v):
        import jax, jax.numpy as jnp
        import numpy as np

        def _wkv(time_decay, time_first, k, v):
            w = -jnp.exp(time_decay)
            u = time_first
            B, T, C = k.shape
            aa = jnp.zeros((B, C), dtype=k.dtype)
            bb = jnp.zeros((B, C), dtype=k.dtype)
            pp = jnp.full((B, C), -1e+38, dtype=k.dtype)

            def step(carry, kv_t):
                aa, bb, pp = carry
                kt, vt = kv_t
                ww = u + kt
                q = jnp.maximum(pp, ww)
                e1 = jnp.exp(pp - q)
                e2 = jnp.exp(ww - q)
                y_t = (e1 * aa + e2 * vt) / (e1 * bb + e2)
                ww2 = pp + w
                q2 = jnp.maximum(ww2, kt)
                e1b = jnp.exp(ww2 - q2)
                e2b = jnp.exp(kt - q2)
                new_carry = (e1b * aa + e2b * vt, e1b * bb + e2b, q2)
                return (new_carry, y_t)
            ks = jnp.transpose(k, (1, 0, 2))
            vs = jnp.transpose(v, (1, 0, 2))
            _, ys = jax.lax.scan(step, (aa, bb, pp), (ks, vs))
            return jnp.transpose(ys, (1, 0, 2))
        assert seq_len <= 128
        return _wkv(time_decay, time_first, k, v)

    def _L0_ffn_ref(x, W1, Wg, W2, Ws1, Wsg, Ws2, gate_w, gate_b, biases):
        import jax, jax.numpy as jnp
        import numpy as np
        NUM_ROUTED = 7
        TOP_K = 3
        D = 256
        H = 256
        B, S = (4, 256)

        def _expert_ffn(x, w1, wg, w2):
            return jax.nn.silu(x @ w1) * (x @ wg) @ w2
        output = _expert_ffn(x, Ws1, Wsg, Ws2)
        gate_logits = x @ gate_w + gate_b
        gate_probas = jax.nn.softmax(gate_logits, axis=-1)
        biased_probas = gate_probas + biases
        _, topk_idxs = jax.lax.top_k(biased_probas, TOP_K)
        topk_probas = jnp.take_along_axis(gate_probas, topk_idxs, axis=-1)
        topk_probas = topk_probas / jnp.sum(topk_probas, axis=-1, keepdims=True)
        for e in range(NUM_ROUTED):
            w_e = jnp.sum(topk_probas * (topk_idxs == e), axis=-1)
            output = output + _expert_ffn(x, W1[e], Wg[e], W2[e]) * w_e[..., None]
        return output
    x = x + _L0_attn_ref(_layernorm(x, axis=-1), L0_attn_wq_codes, L0_attn_wq_scales, L0_attn_bq, L0_attn_wk_codes, L0_attn_wk_scales, L0_attn_bk, L0_attn_wv_codes, L0_attn_wv_scales, L0_attn_bv, L0_attn_wo_codes, L0_attn_wo_scales, L0_attn_bo)
    x = x + _L0_xattn_ref(8, 128, 256, L0_xattn_time_decay, L0_xattn_time_first, _layernorm(x, axis=-1), ctx_2048)
    x = x + _L0_ffn_ref(_layernorm(x, axis=-1), L0_ffn_W1, L0_ffn_Wg, L0_ffn_W2, L0_ffn_Ws1, L0_ffn_Wsg, L0_ffn_Ws2, L0_ffn_gate_w, L0_ffn_gate_b, L0_ffn_biases)
    return x

_drawn_inputs = setup_inputs


def setup_inputs(seed=0):
    import zlib

    import numpy as np

    out = dict(_drawn_inputs(seed))
    spreads = {'L0_attn_bq': (0.0, 0.8),
     'L0_attn_bk': (0.0, 0.8),
     'L0_attn_bv': (0.0, 0.1),
     'L0_attn_bo': (0.0, 0.1),
     'L0_ffn_gate_b': (0.0, 0.8),
     'L0_ffn_biases': (0.0, 0.8)}
    factors = {'L0_attn_wq_scales': 3.166,
     'L0_attn_wk_scales': 3.157,
     'L0_attn_wv_scales': 2.792,
     'L0_ffn_W1': 7.196,
     'L0_ffn_Wg': 7.111,
     'L0_ffn_W2': 7.125,
     'L0_ffn_Ws1': 4.269,
     'L0_ffn_Wsg': 4.235,
     'L0_ffn_Ws2': 4.26,
     'L0_ffn_gate_w': 8.0}
    for name, (base, spread) in spreads.items():
        noise = np.random.default_rng([zlib.crc32(name.encode()), seed]).standard_normal(out[name].shape)
        drawn = base * np.exp(spread * noise) if base else spread * noise
        out[name] = jnp.asarray(drawn.astype(out[name].dtype))
    for name, factor in factors.items():
        out[name] = (out[name] * factor).astype(out[name].dtype)
    return out
```

```python
from contextlib import ExitStack

import concourse.bass as bass
from concourse import mybir

F32 = mybir.dt.float32
F32R = mybir.dt.float32r
ALU = mybir.AluOpType
ACT = mybir.ActivationFunctionType
AX = mybir.AxisListType

P = 128
NB, S, D = 8, 128, 256
HALF = 4
T = HALF * S
NH, DH = 16, 128
KT = D // P
NE, TOPK = 7, 3
EXP = NE + 1
BLK = 32
STEPS = 2 * NH
UNITS = 2 * EXP
PW = KT * 3 * 2 * DH
OW = 2 * D
HW = KT * 2 * D
SEG = S + 1
EPS = 1e-5
EMPTY = -1e38
RESET = -2e38
SCALE = float(DH) ** -0.5

C_BQ, C_BK, C_BV, C_DECAY, C_FIRST, C_GATE = 0, NH, 2 * NH, 3 * NH, 3 * NH + KT, 3 * NH + 2 * KT
C_ALL = C_GATE + KT * NE
R_BO, R_GB, R_BIAS = 0, D, D + NE
R_ALL = D + 2 * NE
PASSES = ((0, 0), (0, 1), (1, 0))


def need(eng, sem, count):
    if not (isinstance(count, int) and count <= 0):
        eng.wait_ge(sem, count)


def live(i, n):
    return not isinstance(i, int) or 0 <= i < n


STAGES = {
    "stats_a": (0, -1), "norm_a": (1, 0), "keys_T": (2, 0), "k_copies": (3, 1), "maxima": (4, 1),
    "decayed": (5, 2), "exponents": (5, 2), "exponentials": (6, 3), "values": (7, 3), "scans": (8, 4),
    "outputs": (9, 5), "outputs_T": (9, 5), "add_y": (10, 6), "norm_b": (11, 7), "x3_T": (11, 7),
    "x3_copies": (12, 8), "gate_logits": (12, 8), "x3_split": (12, 8), "logits": (13, 9),
}
ATTENTION_AT = {0: 2 * 20, 1: 2 * 26}
EXPERTS_AT = {2: 0, 3: 7}
GATE_STEPS = 15


def beside_attention(stages, m, s):
    for pr, first in ATTENTION_AT.items():
        for name, stage in stages.items():
            if STAGES[name][0] + first == 2 * m + s:
                stage(pr)


def beside_experts(stages, u, s):
    for pr, first in EXPERTS_AT.items():
        for name, stage in stages.items():
            if STAGES[name][1] + first == 2 * u + s:
                stage(pr)


def decoder_layer(nc, x_in, ctx_in, wqkv, sqkv, wo, so, wup, wdown, consts, rows, out):
    with ExitStack() as stack:
        def sb(name, shape, dt=F32):
            return stack.enter_context(nc.sbuf_tensor(name, shape, dt))

        def bank(name):
            return stack.enter_context(nc.psum_tensor(name, [P, 512], F32))

        def sem(name):
            return stack.enter_context(nc.semaphore(name))

        x = sb("x", [P, NB, D])
        ctxT = sb("ctxT", [P, KT, NB * S])
        cst = sb("cst", [P, C_ALL])
        row = sb("row", [P, R_ALL])
        ident = sb("ident", [P, P])
        xnT = [[sb(f"xnT{h}{s}", [P, KT, T], F32R) for s in "hl"] for h in range(2)]
        x3T = [[sb(f"x3T{h}{s}", [P, KT, T], F32R) for s in "hl"] for h in range(2)]
        w_st = [sb(f"w_st{i}", [P, PW]) for i in range(2)]
        s_st = [sb(f"s_st{i}", [P, PW]) for i in range(2)]
        wo_st = [sb(f"wo_st{i}", [P, OW]) for i in range(2)]
        so_st = [sb(f"so_st{i}", [P, OW]) for i in range(2)]
        w_s = [[sb(f"w_s{i}{s}", [P, PW], F32R) for s in "hl"] for i in range(2)]
        wo_s = [[sb(f"wo_s{i}{s}", [P, OW], F32R) for s in "hl"] for i in range(2)]
        q_s = [sb(f"q{s}", [P, T], F32R) for s in "hl"]
        k_s = [sb(f"k{s}", [P, T], F32R) for s in "hl"]
        v_sb = [sb(f"v{i}", [P, HALF, 2 * DH]) for i in range(2)]
        e_sb = sb("e_sb", [P, HALF, S])
        pn = sb("pn", [P, HALF, S])
        pT = sb("pT", [P, HALF, S])
        o_s = [sb(f"o{s}", [P, 4, T], F32R) for s in "hl"]
        mx, nmx, rsum, rinv = (sb(n, [P, HALF]) for n in ("mx", "nmx", "rsum", "rinv"))
        st, mv, veps, rstd, lnx = [], [], [], [], []
        for i in range(2):
            st.append(sb(f"st{i}", [P, 2, 6]))
            mv.append(sb(f"mv{i}", [P, 2, 2]))
            veps.append(sb(f"veps{i}", [P, 2]))
            rstd.append(sb(f"rstd{i}", [P, 2]))
            lnx.append(sb(f"lnx{i}", [P, 2, D]))
        mhalf = sb("mhalf", [P, 2])
        segs = lambda name, n=1: sb(name, [P, n * KT * 2, SEG])
        decay, kp, pp, ap, bp, vp = (segs(n) for n in ("decay", "kp", "pp", "ap", "bp", "vp"))
        dd, ee = segs("dd", 4), segs("ee", 4)
        wneg = sb("wneg", [P, KT])
        uk, tq, num, den = (sb(n, [P, KT * 2, S]) for n in ("uk", "tq", "num", "den"))
        x3f = sb("x3f", [P, KT, 2 * S])
        lg = sb("lg", [P, NB, NE])
        g1, g2, gp, gb = (sb(n, [P, HALF, NE]) for n in ("g1", "g2", "gp", "gb"))
        gs = sb("gs", [P, HALF])
        gr = sb("gr", [P, HALF])
        tri = sb("tri", [P, NE, NE])
        r1, r2 = (sb(n, [P, HALF, NE, NE]) for n in ("r1", "r2"))
        we = sb("we", [P, NB, EXP])
        th = sb("th", [P, 2, T])
        hp = sb("hp", [P, 2, T])

        q_ps, k_ps, v_ps, s_ps, t_ps, o_ps, w_ps, aux = (
            bank(n) for n in ("q_ps", "k_ps", "v_ps", "s_ps", "t_ps", "o_ps", "w_ps", "aux"))
        h1_ps, hg_ps, y_ps = [q_ps, v_ps], [k_ps, s_ps], [o_ps, w_ps]

        x_in_s = [sem(f"x_in{h}") for h in range(2)]
        cst_in, row_in, ctx_in_s = sem("cst_in"), sem("row_in"), sem("ctx_in")
        w_in = [sem(f"w_in{i}") for i in range(2)]
        wo_in = [sem(f"wo_in{i}") for i in range(2)]
        stored = sem("stored")
        w_mul, w_hi, w_lo, wo_mul, wo_hi, wo_lo = (sem(n) for n in (
            "w_mul", "w_hi", "w_lo", "wo_mul", "wo_hi", "wo_lo"))
        q_psum, k_psum, v_psum, s_psum, t_psum, o_psum, wo_psum = (sem(n) for n in (
            "q_psum", "k_psum", "v_psum", "s_psum", "t_psum", "o_psum", "wo_psum"))
        q_hi, k_hi, q_lo, k_lo, v_cp, e_done, pt_cp, o_hi, o_lo = (sem(n) for n in (
            "q_hi", "k_hi", "q_lo", "k_lo", "v_cp", "e_done", "pt_cp", "o_hi", "o_lo"))
        s_max, n_max, r_inv, p_norm, wo_add = (sem(n) for n in (
            "s_max", "n_max", "r_inv", "p_norm", "wo_add"))
        ln_st, ln_mv, ln_ve, ln_rs, ln_x = ([sem(f"{n}_{a}") for a in "ab"] for n in (
            "ln_st", "ln_mv", "ln_ve", "ln_rs", "ln_x"))
        ln_T = sem("ln_T")
        xn_hi, xn_lo, x_bo = sem("xn_hi"), sem("xn_lo"), sem("x_bo")
        idn, consts_done, pads, wneg_s, dec_s = (sem(n) for n in (
            "idn", "consts_done", "pads", "wneg", "dec"))
        k_cp, uk_cp, p_scan, t_cp, q_max, d_sub, e_exp, v_mul, a_scan, b_scan = (sem(n) for n in (
            "k_cp", "uk_cp", "p_scan", "t_cp", "q_max", "d_sub", "e_exp", "v_mul", "a_scan", "b_scan"))
        n1_s, n2_s, d1_s, num_s, den_s, rec_s, y_s, y_psum, x2_s = (sem(n) for n in (
            "n1", "n2", "d1", "num_s", "den_s", "rec_s", "y_s", "y_psum", "x2_s"))
        x3_psum, x3_cp, x3_hi, x3_lo, lg_psum, lg_s = (sem(n) for n in (
            "x3_psum", "x3_cp", "x3_hi", "x3_lo", "lg_psum", "lg_s"))
        g_step, g_exp, g_done = sem("g_step"), sem("g_exp"), sem("g_done")
        h1_psum, hg_psum, th_s, a_s, h_s, h_hi, h_lo, y2_psum, acc = (sem(n) for n in (
            "h1_psum", "hg_psum", "th_s", "a_s", "h_s", "h_hi", "h_lo", "y2_psum", "acc"))

        def qkv(i, s, kt, mat, a, b):
            at = (kt * 3 + mat) * 2 * DH
            return w_s[i][s][:, at + a:at + b]

        def up(i, s, kt, mat, mt):
            at = (kt * 2 + mat) * D + mt * P
            return w_s[i][s][:, at:at + P]

        def seg(t, i=0):
            return t[:, i * 2 * KT:(i + 1) * 2 * KT, 1:SEG]

        def before(t, i=0):
            return t[:, i * 2 * KT:(i + 1) * 2 * KT, 0:S]

        def flat(t, i=0):
            return t[:, i * 2 * KT:(i + 1) * 2 * KT, :].rearrange("p s t -> p (s t)")

        def b_bank(pr):
            return aux if pr < 2 else t_ps

        block = stack.enter_context(nc.Block())

        @block.sync
        def _(sp):
            def by_block(scales):
                rows_, n = scales.shape
                return scales.rearrange("b (o n) -> b o n", o=1).broadcast_to([rows_, BLK, n])

            def load_w(p, i, g):
                need(sp, w_lo, p - 1)
                sp.dma_start(w_st[i][:], wqkv[g]).then_inc(w_in[i], 16)
                sp.dma_start(s_st[i][:], by_block(sqkv[g])).then_inc(w_in[i], 16)

            def load_wo(p, i, g):
                need(sp, wo_lo, p - 1)
                sp.dma_start(wo_st[i][:], wo[g]).then_inc(wo_in[i], 16)
                sp.dma_start(so_st[i][:], by_block(so[g])).then_inc(wo_in[i], 16)

            def load_up(u, i, e):
                need(sp, w_lo, NH + u - 1)
                sp.dma_start(w_st[i][:, 0:HW], wup[e]).then_inc(w_in[i], 16)

            def load_down(u, i, e):
                need(sp, wo_lo, NH + u - 1)
                sp.dma_start(wo_st[i][:], wdown[e]).then_inc(wo_in[i], 16)

            sp.dma_start(x[:, 0:HALF, :], x_in[:, 0:HALF, :]).then_inc(x_in_s[0], 16)
            load_w(0, 0, 0)
            sp.dma_start(cst[:], consts).then_inc(cst_in, 16)
            sp.dma_start(row[:], rows.broadcast_to([P, R_ALL])).then_inc(row_in, 16)
            sp.dma_start(x[:, HALF:NB, :], x_in[:, HALF:NB, :]).then_inc(x_in_s[1], 16)
            load_w(1, 1, 1)
            load_wo(0, 0, 0)
            for h in range(2):
                with sp.Fori(0, 3) as t:
                    for k in range(2):
                        load_w(8 * h + 2 * t + 2 + k, k, 2 * t + 2 + k)
                        load_wo(8 * h + 2 * t + 1 + k, (1 + k) % 2, 2 * t + 1 + k)
                if h == 0:
                    sp.dma_start(ctxT[:], ctx_in).then_inc(ctx_in_s, 16)
                    load_w(8, 0, 0)
                    load_wo(7, 1, 7)
                    load_w(9, 1, 1)
                    load_wo(8, 0, 0)
            load_up(0, 0, 0)
            load_wo(15, 1, 7)
            load_up(1, 1, 1)
            load_down(0, 0, 0)
            for h in range(2):
                with sp.Fori(0, 3) as t:
                    for k in range(2):
                        load_up(8 * h + 2 * t + 2 + k, k, 2 * t + 2 + k)
                        load_down(8 * h + 2 * t + 1 + k, (1 + k) % 2, 2 * t + 1 + k)
                if h == 0:
                    load_up(8, 0, 0)
                    load_down(7, 1, 7)
                    load_up(9, 1, 1)
                    load_down(8, 0, 0)
                else:
                    load_down(15, 1, 7)
            sp.wait_ge(acc, 2 * EXP)
            sp.dma_start(out[:, 0:HALF, :], x[:, 0:HALF, :]).then_inc(stored, 16)
            for bb in range(2):
                sp.wait_ge(acc, 4 * EXP - 1 + bb)
                b = HALF + 2 * bb
                sp.dma_start(out[:, b:b + 2, :], x[:, b:b + 2, :]).then_inc(stored, 16)
            sp.wait_ge(stored, 3 * 16)

        @block.gpsimd
        def _(pool):
            def mul_w(p, i, it):
                need(pool, w_in[i], 32 * (it + 1))
                pool.tensor_tensor(w_st[i][:], w_st[i][:], s_st[i][:], ALU.mult).then_inc(w_mul, 1)

            def lo_w(p, i, n=PW):
                need(pool, w_hi, p + 1)
                pool.tensor_tensor(w_s[i][1][:, 0:n], w_st[i][:, 0:n], w_s[i][0][:, 0:n].bitcast(F32),
                                   ALU.subtract).then_inc(w_lo, 1)

            def mul_wo(p, i, it):
                need(pool, wo_in[i], 32 * (it + 1))
                pool.tensor_tensor(wo_st[i][:], wo_st[i][:], so_st[i][:], ALU.mult).then_inc(wo_mul, 1)

            def lo_wo(p, i):
                need(pool, wo_hi, p + 1)
                pool.tensor_tensor(wo_s[i][1][:], wo_st[i][:], wo_s[i][0][:].bitcast(F32),
                                   ALU.subtract).then_inc(wo_lo, 1)

            def rstd_of(a, k):
                need(pool, ln_ve[a], k + 1)
                need(pool, ln_x[a], k)
                pool.tensor_tensor(rstd[a][:], veps[a][:], mhalf[:], ALU.pow).then_inc(ln_rs[a], 1)

            def add_bo(pr, b):
                need(pool, ln_x[0], pr + 1)
                if pr == 0:
                    pool.wait_ge(row_in, 16)
                bo = row[:, R_BO:R_BO + D].rearrange("p (o d) -> p o d", o=1).broadcast_to([P, 2, D])
                pool.tensor_tensor(x[:, b:b + 2, :], x[:, b:b + 2, :], bo, ALU.add).then_inc(x_bo, 1)

            def exponents(pr):
                need(pool, q_max, pr + 1)
                need(pool, t_cp, pr + 1)
                need(pool, e_exp, pr)
                sub = ALU.subtract
                pool.tensor_tensor(seg(dd, 0), before(pp), seg(ap), sub)
                pool.tensor_tensor(seg(dd, 1), uk[:], seg(ap), sub)
                pool.tensor_tensor(seg(dd, 2), tq[:], seg(pp), sub)
                pool.tensor_tensor(seg(dd, 3), seg(kp), seg(pp), sub).then_inc(d_sub, 1)

            def values(pr):
                b = 2 * pr
                if pr == 0:
                    pool.wait_ge(ctx_in_s, 16)
                need(pool, e_exp, pr + 1)
                for ct in range(KT):
                    v = ctxT[:, ct, b * S:(b + 2) * S].rearrange("p (b t) -> p b t", b=2)
                    i = pool.tensor_tensor(vp[:, 2 * ct:2 * ct + 2, 1:SEG],
                                           ee[:, 6 * KT + 2 * ct:6 * KT + 2 * ct + 2, 1:SEG], v, ALU.mult)
                i.then_inc(v_mul, 1)
                need(pool, y_s, pr)
                for ct in range(KT):
                    v = ctxT[:, ct, b * S:(b + 2) * S].rearrange("p (b t) -> p b t", b=2)
                    i = pool.tensor_tensor(num[:, 2 * ct:2 * ct + 2, :],
                                           ee[:, 2 * KT + 2 * ct:2 * KT + 2 * ct + 2, 1:SEG], v, ALU.mult)
                i.then_inc(n2_s, 1)
                need(pool, a_scan, pr + 1)
                pool.tensor_tensor(uk[:], seg(ee, 0), before(ap), ALU.mult).then_inc(n1_s, 1)
                need(pool, b_scan, pr + 1)
                need(pool, rec_s, pr)
                pool.tensor_tensor(den[:], seg(ee, 0), before(bp), ALU.mult).then_inc(d1_s, 1)

            def lo_x3(pr):
                h, c = pr // 2, 2 * S * (pr % 2)
                need(pool, x3_hi, pr + 1)
                pool.tensor_tensor(x3T[h][1][:, :, c:c + 2 * S], x3f[:],
                                   x3T[h][0][:, :, c:c + 2 * S].bitcast(F32),
                                   ALU.subtract).then_inc(x3_lo, 1)

            def lo_h(u, mt, k):
                need(pool, h_hi, 2 * u + mt + 1)
                pool.tensor_tensor(o_s[1][:, 2 * k + mt, :], hp[:, mt, :],
                                   o_s[0][:, 2 * k + mt, :].bitcast(F32), ALU.subtract).then_inc(h_lo, 1)

            pool.memset(mhalf[:], -0.5).then_inc(idn, 1)
            pool.memset(ident[:], 0.0).then_inc(idn, 1)
            pool.memset(tri[:], 1.0).then_inc(idn, 1)
            pool.wait_ge(idn, 3)
            pool.affine_select(out=ident[:], in_=ident[:], compare_op=ALU.not_equal, fill=1.0, base=0,
                               pattern=[[-1, P]], channel_multiplier=1).then_inc(idn, 1)
            pool.affine_select(out=tri[:], in_=tri[:], compare_op=ALU.is_gt, fill=0.0, base=0,
                               pattern=[[1, NE], [-1, NE]], channel_multiplier=0).then_inc(idn, 1)
            mul_w(0, 0, 0)
            rstd_of(0, 0)
            rstd_of(0, 1)
            lo_w(0, 0)
            mul_w(1, 1, 0)
            add_bo(0, 0)
            add_bo(1, 2)
            mul_wo(0, 0, 0)

            def turn(it, sides=None):
                for k in range(2):
                    p = 2 * it + 1 + k
                    lo_w(p, (1 + k) % 2, HW if isinstance(p, int) and p == NH else PW)
                    if sides:
                        sides(4 * it + 2 * k, 0)
                    if live(p + 1, NH):
                        mul_w(p + 1, k % 2, it + 1)
                    if sides:
                        sides(4 * it + 2 * k, 1)
                    lo_wo(p - 1, k)
                    if sides:
                        sides(4 * it + 2 * k + 1, 0)
                    if live(p, NH):
                        mul_wo(p, (1 + k) % 2, it + k)
                    if sides:
                        sides(4 * it + 2 * k + 1, 1)

            def first_norms(m, s):
                if m < 2 and s == 0:
                    rstd_of(0, 2 + m)
                elif m < 2:
                    add_bo(2 + m, HALF + 2 * m)

            stages = {
                "stats_a": lambda pr: rstd_of(0, 4 + pr), "exponents": exponents, "values": values,
                "add_y": lambda pr: rstd_of(1, pr), "x3_split": lo_x3,
            }
            turn(0, first_norms)
            with pool.Fori(1, 4) as it:
                turn(it)
            turn(4)
            for t in range(5, 8):
                turn(t, lambda m, s: beside_attention(stages, m, s))
            beside_attention(stages, STEPS, 0)
            beside_attention(stages, STEPS, 1)
            stages["stats_a"](2)

            def unit(u, k, sides=None):
                if live(u + 1, UNITS):
                    lo_w(NH + u + 1, (k + 1) % 2, HW)
                lo_wo(NH + u, k)
                if sides:
                    sides(u, 0)
                for mt in range(2):
                    lo_h(u, mt, k)
                if sides:
                    sides(u, 1)

            for u in range(EXP):
                unit(u, u % 2, lambda u, s: beside_experts(stages, u, s))
            beside_experts(stages, EXP, 0)
            unit(8, 0)
            unit(9, 1)
            with pool.Fori(5, 7) as t:
                for k in range(2):
                    unit(2 * t + k, k)
            unit(14, 0)
            unit(15, 1)

        @block.scalar
        def _(act):
            def ln1_hi(pr, h, hp_):
                need(act, ln_T, pr + 1)
                act.copy(xnT[h][0][:, :, 2 * S * hp_:2 * S * (hp_ + 1)],
                         aux[:].rearrange("p (k t) -> p k t", k=KT)).then_inc(xn_hi, 1)

            def softmax_exp(n):
                need(act, n_max, n + 1)
                need(act, p_norm, n)
                for b in range(HALF):
                    i = act.activation(e_sb[:, b, :], s_ps[:, b * S:(b + 1) * S], ACT.Exp, bias=nmx[:, b:b + 1],
                                       scale=SCALE, accum_out=rsum[:, b:b + 1])
                i.then_inc(e_done, 1)

            def hi_of(n, ps, dst, bias, ready, done, used):
                need(act, ready, n + 1)
                need(act, used, n)
                act.activation(dst, ps[:], ACT.Identity, bias=bias).then_inc(done, 1)

            def k_copies(pr):
                need(act, ln_T, 4 + pr + 1)
                need(act, y_psum, pr)
                act.copy(seg(kp), aux[:].rearrange("p (s t) -> p s t", t=S)).then_inc(k_cp, 1)
                for ct in range(KT):
                    i = act.activation(uk[:, 2 * ct:2 * ct + 2, :],
                                       aux[:, 2 * S * ct:2 * S * (ct + 1)].rearrange("p (s t) -> p s t", t=S),
                                       ACT.Identity, bias=cst[:, C_FIRST + ct:C_FIRST + ct + 1])
                i.then_inc(uk_cp, 1)

            def decayed(pr):
                need(act, p_scan, pr + 1)
                if pr == 0:
                    act.wait_ge(dec_s, 1)
                for ct in range(KT):
                    i = act.activation(tq[:, 2 * ct:2 * ct + 2, :], pp[:, 2 * ct:2 * ct + 2, 0:S],
                                       ACT.Identity, bias=wneg[:, ct:ct + 1])
                i.then_inc(t_cp, 1)

            def exponentials(pr):
                need(act, d_sub, pr + 1)
                act.activation(ee[:, :, 1:SEG], dd[:, :, 1:SEG], ACT.Exp).then_inc(e_exp, 1)

            def x3_copies(pr):
                h, c = pr // 2, 2 * S * (pr % 2)
                need(act, x3_psum, pr + 1)
                need(act, x3_lo, pr)
                act.copy(x3f[:], b_bank(pr)[:].rearrange("p (k t) -> p k t", k=KT)).then_inc(x3_cp, 1)
                act.wait_ge(x3_cp, pr + 1)
                act.copy(x3T[h][0][:, :, c:c + 2 * S], x3f[:]).then_inc(x3_hi, 1)

            act.wait_ge(cst_in, 16)
            act.activation(wneg[:], cst[:, C_DECAY:C_DECAY + KT], ACT.Exp).then_inc(wneg_s, 1)
            ln1_hi(0, 0, 0)
            ln1_hi(1, 0, 1)

            def step(it, j, half, sides=None):
                m = 4 * it + j
                head = lambda i: i % NH if isinstance(i, int) else i - NH * half
                if live(m - 1, STEPS):
                    softmax_exp(m - 1)
                if live(m - 2, STEPS):
                    n = m - 2
                    hi_of(n, o_ps, o_s[0][:, (j - 2) % 4, :], cst[:, bass.ds(C_BV + head(n), 1)],
                          o_psum, o_hi, o_lo)
                if live(m, STEPS):
                    hi_of(m, q_ps, q_s[0][:], cst[:, bass.ds(C_BQ + head(m), 1)], q_psum, q_hi, q_lo)
                    hi_of(m, k_ps, k_s[0][:], cst[:, bass.ds(C_BK + head(m), 1)], k_psum, k_hi, k_lo)
                    need(act, v_psum, m + 1)
                    b = 2 * (j % 2)
                    act.copy(v_sb[j // 2 % 2][:, b:b + 2, :],
                             v_ps[:].rearrange("p (b f) -> p b f", b=2)).then_inc(v_cp, 1)
                if sides:
                    sides(0)
                if live(m - 1, STEPS):
                    need(act, t_psum, m)
                    act.copy(pT[:], t_ps[:].rearrange("p (b f) -> p b f", b=HALF)).then_inc(pt_cp, 1)
                if sides:
                    sides(1)

            def turn(it, half, sides=None):
                for j in range(4):
                    step(it, j, half)
                    if sides:
                        sides(j)

            def first_norms(j):
                if j in (1, 2):
                    ln1_hi(1 + j, 1, j - 1)

            stages = {"k_copies": k_copies, "decayed": decayed, "exponentials": exponentials,
                      "x3_copies": x3_copies}
            turn(0, 0, first_norms)
            with act.Fori(1, 4) as it:
                turn(it, 0)
            turn(4, 1)
            for m in range(20, STEPS + 2):
                step(m // 4, m % 4, 1, lambda s: beside_attention(stages, m, s))

            def gate_exp(h):
                act.wait_ge(g_step, GATE_STEPS * h + 2)
                act.activation(gp[:], g1[:], ACT.Exp).then_inc(g_exp, 1)

            def unit(u, k, sides=None):
                for mt in range(2):
                    r = 2 * u + mt
                    need(act, h1_psum, r + 1)
                    need(act, h_s, r - 1)
                    act.activation(th[:, mt, :], h1_ps[mt][:], ACT.Tanh, scale=0.5).then_inc(th_s, 1)
                if sides:
                    sides(0)
                for mt in range(2):
                    need(act, h_s, 2 * u + mt + 1)
                    need(act, y2_psum, 2 * u - 2)
                    if isinstance(u, int) and u < 2:
                        act.wait_ge(wo_psum, STEPS)
                    act.copy(o_s[0][:, 2 * k + mt, :], hp[:, mt, :]).then_inc(h_hi, 1)
                if sides:
                    sides(1)

            gate_exp(0)
            for u in range(EXP):
                unit(u, u % 2, lambda s: beside_experts(stages, u, s))
            beside_experts(stages, EXP, 0)
            gate_exp(1)
            unit(8, 0)
            unit(9, 1)
            with act.Fori(5, 8) as t:
                for k in range(2):
                    unit(2 * t + k, k)

        @block.vector
        def _(dve):
            sub, mult, add = ALU.subtract, ALU.mult, ALU.add

            def stats(a, k, b):
                need(dve, ln_mv[a], k)
                for i in range(2):
                    s = dve.bn_stats(st[a][:, i, :], x[:, b + i, :])
                s.then_inc(ln_st[a], 1)
                dve.wait_ge(ln_st[a], k + 1)
                need(dve, ln_x[a], k)
                for i in range(2):
                    s = dve.bn_aggr(mv[a][:, i, :], st[a][:, i, :])
                s.then_inc(ln_mv[a], 1)
                dve.wait_ge(ln_mv[a], k + 1)
                need(dve, ln_rs[a], k)
                dve.tensor_scalar(veps[a][:], mv[a][:, :, 1], EPS, None, add).then_inc(ln_ve[a], 1)

            def normalised(a, k, b):
                need(dve, ln_rs[a], k + 1)
                need(dve, x3_psum if a else ln_T, k)
                for i in range(2):
                    s = dve.tensor_scalar(lnx[a][:, i, :], x[:, b + i, :], mv[a][:, i, 0:1],
                                          rstd[a][:, i:i + 1], sub, mult)
                s.then_inc(ln_x[a], 1)

            def ln1_lo(pr, h, hp_):
                need(dve, xn_hi, pr + 1)
                c = slice(2 * S * hp_, 2 * S * (hp_ + 1))
                dve.tensor_tensor(xnT[h][1][:, :, c], aux[:].rearrange("p (k t) -> p k t", k=KT),
                                  xnT[h][0][:, :, c].bitcast(F32), sub).then_inc(xn_lo, 1)

            def hi_w(p, i, n=PW):
                if isinstance(p, int) and p >= NH:
                    dve.wait_ge(w_in[i], 32 * (NH // 2) + 16 * ((p - NH) // 2 + 1))
                else:
                    need(dve, w_mul, p + 1)
                dve.tensor_copy(w_s[i][0][:, 0:n], w_st[i][:, 0:n]).then_inc(w_hi, 1)

            def hi_wo(p, i):
                dve.tensor_copy(wo_s[i][0][:], wo_st[i][:]).then_inc(wo_hi, 1)

            def add_out(w, j, half):
                need(dve, wo_psum, w + 1)
                if isinstance(w, int):
                    half = w // NH
                    if w < 2:
                        dve.wait_ge(x_bo, 4)
                need(dve, wo_add, w)
                b = HALF * half + 2 * (j % 2)
                xb = x[:, b:b + 2, :]
                dve.tensor_tensor(xb, w_ps[:].rearrange("p (b d) -> p b d", b=2), xb, add).then_inc(wo_add, 1)

            def softmax_max(n):
                need(dve, s_psum, n + 1)
                need(dve, n_max, n)
                dve.tensor_reduce(mx[:], s_ps[:].rearrange("p (b k) -> p b k", b=HALF), AX.X,
                                  ALU.max).then_inc(s_max, 1)
                dve.wait_ge(s_max, n + 1)
                need(dve, e_done, n)
                dve.tensor_scalar(nmx[:], mx[:], -SCALE, None, mult).then_inc(n_max, 1)

            def softmax_norm(n):
                need(dve, e_done, n + 1)
                need(dve, p_norm, n)
                dve.reciprocal(rinv[:], rsum[:]).then_inc(r_inv, 1)
                dve.wait_ge(r_inv, n + 1)
                need(dve, t_psum, n)
                ri = rinv[:].rearrange("p (b o) -> p b o", o=1).broadcast_to([P, HALF, S])
                dve.tensor_tensor(pn[:], e_sb[:], ri, mult).then_inc(p_norm, 1)

            def lo_of(n, ps, hi, lo, bias, ready, done):
                need(dve, ready, n + 1)
                dve.scalar_tensor_tensor(lo, ps[:], bias, hi.bitcast(F32), add, sub).then_inc(done, 1)

            def maxima(pr):
                need(dve, uk_cp, pr + 1)
                if isinstance(pr, int) and pr == 0:
                    dve.wait_ge(pads, 1)
                dve.tensor_tensor_scan(flat(pp), flat(decay), flat(kp), 0.0, add, ALU.max).then_inc(p_scan, 1)
                dve.wait_ge(p_scan, pr + 1)
                need(dve, n1_s, pr)
                dve.tensor_tensor(seg(ap), before(pp), uk[:], ALU.max).then_inc(q_max, 1)

            def scans(pr):
                need(dve, v_mul, pr + 1)
                dve.tensor_tensor_scan(flat(ap), flat(ee, 2), flat(vp), 0.0, mult, add).then_inc(a_scan, 1)
                dve.tensor_tensor_scan(flat(bp), flat(ee, 2), flat(ee, 3), 0.0, mult, add).then_inc(b_scan, 1)

            def outputs(pr):
                need(dve, n1_s, pr + 1)
                dve.tensor_tensor(num[:], num[:], uk[:], add).then_inc(num_s, 1)
                need(dve, d1_s, pr + 1)
                dve.tensor_tensor(den[:], den[:], seg(ee, 1), add).then_inc(den_s, 1)
                dve.wait_ge(den_s, pr + 1)
                dve.reciprocal(tq[:], den[:]).then_inc(rec_s, 1)
                dve.wait_ge(rec_s, pr + 1)
                need(dve, y_psum, pr)
                dve.tensor_tensor(uk[:], num[:], tq[:], mult).then_inc(y_s, 1)

            def add_y(pr):
                b = 2 * pr
                need(dve, y_psum, pr + 1)
                for i in range(2):
                    s = dve.tensor_tensor(x[:, b + i, :], b_bank(pr)[:, D * i:D * (i + 1)], x[:, b + i, :], add)
                s.then_inc(x2_s, 1)
                dve.wait_ge(x2_s, pr + 1)
                stats(1, pr, b)

            def logits(pr):
                b = 2 * pr
                need(dve, lg_psum, pr + 1)
                for i in range(2):
                    s = dve.tensor_tensor(lg[:, b + i, :], b_bank(pr)[:, NE * i:NE * (i + 1)], row[:, R_GB:R_GB + NE],
                                          add)
                s.then_inc(lg_s, 1)

            dve.wait_ge(x_in_s[0], 16)
            stats(0, 0, 0)
            dve.wait_ge(idn, 5)
            normalised(0, 0, 0)
            stats(0, 1, 2)
            normalised(0, 1, 2)
            hi_w(0, 0)
            ln1_lo(0, 0, 0)
            ln1_lo(1, 0, 1)
            hi_w(1, 1)
            dve.memset(we[:], 1.0).then_inc(consts_done, 1)
            for t, v in ((decay, 0.0), (kp, EMPTY), (vp, 0.0), (ee, 0.0)):
                dve.memset(t[:], v).then_inc(consts_done, 1)
            dve.wait_ge(wneg_s, 1)
            dve.wait_ge(row_in, 16)
            dve.wait_ge(cst_in, 16)
            dve.tensor_scalar(wneg[:], wneg[:], -1.0, None, mult).then_inc(dec_s, 1)
            dve.wait_ge(dec_s, 1)
            dve.wait_ge(consts_done, 5)
            for ct in range(KT):
                c = decay[:, 2 * ct:2 * ct + 2, 1:SEG]
                dve.tensor_scalar(c, c, wneg[:, ct:ct + 1], None, add)
            dve.memset(decay[:, :, 0], RESET).then_inc(pads, 1)

            def step(it, j, half, sides=None):
                m = 4 * it + j
                head = lambda i: i % NH if isinstance(i, int) else i - NH * half
                if live(m - 1, STEPS):
                    softmax_max(m - 1)
                if live(m - 4, STEPS):
                    add_out(m - 4, j, half)
                if live(m - 1, STEPS):
                    softmax_norm(m - 1)
                if sides:
                    sides(m, 0)
                if live(m - 2, STEPS):
                    n, i = m - 2, (j - 2) % 4
                    lo_of(n, o_ps, o_s[0][:, i, :], o_s[1][:, i, :], cst[:, bass.ds(C_BV + head(n), 1)],
                          o_hi, o_lo)
                if live(m, STEPS):
                    lo_of(m, q_ps, q_s[0][:], q_s[1][:], cst[:, bass.ds(C_BQ + head(m), 1)], q_hi, q_lo)
                    lo_of(m, k_ps, k_s[0][:], k_s[1][:], cst[:, bass.ds(C_BK + head(m), 1)], k_hi, k_lo)
                    if j % 2:
                        p = 2 * it + (j + 3) // 2
                        if live(p, NH):
                            need(dve, v_psum, m + 1)
                            hi_w(p, (j + 3) // 2 % 2)
                    else:
                        p = 2 * it + j // 2
                        need(dve, wo_mul, p + 1)
                        need(dve, wo_psum, 2 * p - 2)
                        hi_wo(p, j // 2 % 2)

                if sides:
                    sides(m, 1)

            def first_norms(j, s):
                if s == 0 and j < 2:
                    dve.wait_ge(x_in_s[1], 16)
                    stats(0, 2 + j, HALF + 2 * j)
                elif s == 1:
                    if j < 2:
                        normalised(0, 2 + j, HALF + 2 * j)
                    if j in (1, 2):
                        ln1_lo(1 + j, 1, j - 1)

            def stats_a(pr):
                dve.wait_ge(wo_add, NH * (pr // 2 + 1))
                stats(0, 4 + pr, 2 * pr)

            stages = {
                "stats_a": stats_a, "norm_a": lambda pr: normalised(0, 4 + pr, 2 * pr), "maxima": maxima,
                "scans": scans, "outputs": outputs, "add_y": add_y,
                "norm_b": lambda pr: normalised(1, pr, 2 * pr), "logits": logits,
            }
            for j in range(4):
                step(0, j, 0, first_norms)
            with dve.Fori(1, 4) as it:
                for j in range(4):
                    step(it, j, 0)
            for j in range(4):
                step(4, j, 1)
            for m in range(20, STEPS + 4):
                if m == STEPS - 2:
                    dve.wait_ge(v_psum, STEPS - 2)
                    hi_w(NH, 0, HW)
                step(m // 4, m % 4, 1, lambda m, s: beside_attention(stages, m, s))
            stages["stats_a"](2)

            def gate(h):
                c = slice(HALF * h, HALF * (h + 1))
                cast = lambda t: t.rearrange("p (b o) -> p b o", o=1).broadcast_to([P, HALF, NE])
                count = [GATE_STEPS * h]

                def then(i):
                    count[0] += 1
                    i.then_inc(g_step, 1)
                    dve.wait_ge(g_step, count[0])

                dve.wait_ge(lg_s, 2 * (h + 1))
                then(dve.tensor_reduce(gs[:], lg[:, c, :], AX.X, ALU.max))
                then(dve.tensor_tensor(g1[:], lg[:, c, :], cast(gs[:]), sub))
                dve.wait_ge(g_exp, h + 1)
                then(dve.tensor_reduce(gs[:], gp[:], AX.X, add))
                then(dve.reciprocal(gr[:], gs[:]))
                then(dve.tensor_tensor(g2[:], gp[:], cast(gr[:]), mult))
                bias = row[:, R_BIAS:R_BIAS + NE].rearrange("p (o e) -> p o e", o=1).broadcast_to([P, HALF, NE])
                then(dve.tensor_tensor(gb[:], g2[:], bias, add))
                other = gb[:].rearrange("p b (o j) -> p b o j", o=1).broadcast_to([P, HALF, NE, NE])
                own = gb[:].rearrange("p b (e o) -> p b e o", o=1).broadcast_to([P, HALF, NE, NE])
                before_ = tri[:].rearrange("p (o e) j -> p o e j", o=1).broadcast_to([P, HALF, NE, NE])
                then(dve.tensor_tensor(r1[:], other, own, ALU.is_gt))
                then(dve.tensor_tensor(r2[:], other, own, ALU.is_equal))
                then(dve.tensor_tensor(r2[:], r2[:], before_, mult))
                then(dve.tensor_tensor(r1[:], r1[:], r2[:], add))
                then(dve.tensor_reduce(g1[:], r1[:], AX.X, add))
                then(dve.scalar_tensor_tensor(g1[:], g1[:], float(TOPK), g2[:], ALU.is_lt, mult))
                then(dve.tensor_reduce(gs[:], g1[:], AX.X, add))
                then(dve.reciprocal(gr[:], gs[:]))
                dve.wait_ge(consts_done, 5)
                then(dve.tensor_tensor(we[:, c, 0:NE], g1[:], cast(gr[:]), mult))

            def add_expert(u, half):
                for bb in range(2):
                    need(dve, y2_psum, 2 * u + bb + 1)
                    need(dve, acc, 2 * u + bb - 1)
                    for i in range(2):
                        b = HALF * half + 2 * bb + i
                        e = u - EXP * half
                        s = dve.scalar_tensor_tensor(x[:, b, :], y_ps[bb][:, D * i:D * (i + 1)],
                                                     we[:, b, bass.ds(e, 1)], x[:, b, :], mult, add)
                    s.then_inc(acc, 1)

            def loaded(t):
                return 32 * (NH // 2) + 16 * (t + 1)

            def unit(t, k, half, sides=None):
                u, n = 2 * t + k, (k + 1) % 2
                if live(u + 1, UNITS):
                    dve.wait_ge(w_in[n], loaded(t + k))
                    need(dve, hg_psum, 2 * u)
                    if isinstance(u, int) and u == 0:
                        dve.wait_ge(v_psum, STEPS)
                    dve.tensor_copy(w_s[n][0][:, 0:HW], w_st[n][:, 0:HW]).then_inc(w_hi, 1)
                dve.wait_ge(wo_in[k], loaded(t))
                if isinstance(u, int) and u < 2:
                    dve.wait_ge(wo_psum, STEPS - 2 + 2 * u)
                need(dve, y2_psum, 2 * u - 2)
                hi_wo(NH + u, k)
                if live(u - 2, UNITS):
                    add_expert(u - 2, (u - 2) // EXP if isinstance(u, int) else half)
                if sides:
                    sides(u, 0)
                for mt in range(2):
                    r = 2 * u + mt
                    need(dve, th_s, r + 1)
                    dve.scalar_tensor_tensor(th[:, mt, :], th[:, mt, :], 1.0, h1_ps[mt][:], add,
                                             mult).then_inc(a_s, 1)
                    dve.wait_ge(a_s, r + 1)
                    need(dve, hg_psum, r + 1)
                    need(dve, h_lo, r - 1)
                    dve.scalar_tensor_tensor(hp[:, mt, :], th[:, mt, :], 0.5, hg_ps[mt][:], mult,
                                             mult).then_inc(h_s, 1)
                if sides:
                    sides(u, 1)

            gate(0)
            for u in range(EXP):
                unit(u // 2, u % 2, 0, lambda u, s: beside_experts(stages, u, s))
            beside_experts(stages, EXP, 0)
            gate(1)
            unit(4, 0, 1)
            unit(4, 1, 1)
            with dve.Fori(5, 7) as t:
                for k in range(2):
                    unit(t, k, 1)
            unit(7, 0, 1)
            unit(7, 1, 1)
            add_expert(14, 1)
            add_expert(15, 1)

        @block.tensor
        def _(pe):
            def split_mm(out_, pairs):
                every = [(l[a], r[b]) for l, r in pairs for a, b in PASSES]
                for i, (l, r) in enumerate(every):
                    mm = pe.matmul(out_, l, r, start=i == 0, stop=i == len(every) - 1)
                return mm

            def ln_transpose(a, k, bank_):
                need(pe, ln_x[a], k + 1)
                for kt in range(KT):
                    for b in range(2):
                        at = (2 * kt + b) * S
                        mm = pe.transpose(bank_[:, at:at + S], lnx[a][:, b, kt * P:(kt + 1) * P], ident[:])
                return mm

            def ln1_T(pr):
                need(pe, xn_lo, pr)
                ln_transpose(0, pr, aux).then_inc(ln_T, 1)

            def scores(n):
                need(pe, q_lo, n + 1)
                need(pe, k_lo, n + 1)
                need(pe, e_done, n)
                for b in range(HALF):
                    c = slice(b * S, (b + 1) * S)
                    mm = split_mm(s_ps[:, c], [([t[:, c] for t in q_s], [t[:, c] for t in k_s])])
                mm.then_inc(s_psum, 1)

            def attend(n, j, vcount):
                need(pe, pt_cp, n + 1)
                need(pe, v_cp, vcount)
                need(pe, o_lo, n)
                i, f = j // 2, (j % 2) * DH
                for b in range(HALF):
                    mm = pe.matmul(o_ps[:, b * S:(b + 1) * S], v_sb[i][:, b, f:f + DH], pT[:, b, :],
                                   start=True, stop=True)
                mm.then_inc(o_psum, 1)

            def project(m, j, half, pair):
                i, f = j // 2, (j % 2) * DH
                xs = xnT[half]
                need(pe, w_lo, pair + 1)
                need(pe, xn_lo, 2 * (half + 1))
                for mat, ps, ready, used in ((0, q_ps, q_psum, q_lo), (1, k_ps, k_psum, k_lo)):
                    need(pe, used, m)
                    split_mm(ps[:], [([qkv(i, s, kt, mat, f, f + DH) for s in range(2)],
                                      [xs[s][:, kt, :] for s in range(2)]) for kt in range(KT)]).then_inc(ready, 1)
                need(pe, v_cp, m)
                for b in range(2):
                    t = (2 * (j % 2) + b) * S
                    mm = split_mm(v_ps[:, 2 * DH * b:2 * DH * (b + 1)],
                                  [([xs[s][:, kt, t:t + S] for s in range(2)],
                                    [qkv(i, s, kt, 2, 0, 2 * DH) for s in range(2)]) for kt in range(KT)])
                mm.then_inc(v_psum, 1)

            def prob_T(n):
                need(pe, p_norm, n + 1)
                need(pe, pt_cp, n)
                for b in range(HALF):
                    mm = pe.transpose(t_ps[:, b * S:(b + 1) * S], pn[:, b, :], ident[:])
                mm.then_inc(t_psum, 1)

            def project_out(w, j, pair):
                need(pe, o_lo, 2 * pair + 2)
                need(pe, wo_lo, pair + 1)
                need(pe, wo_add, w)
                i = j // 2
                for b in range(2):
                    t = (2 * (j % 2) + b) * S
                    mm = split_mm(w_ps[:, D * b:D * (b + 1)],
                                  [([o_s[s][:, 2 * i + h, t:t + S] for s in range(2)],
                                    [wo_s[i][s][:, D * h:D * (h + 1)] for s in range(2)]) for h in range(2)])
                mm.then_inc(wo_psum, 1)

            def step(it, j, half, sides=None):
                m = 4 * it + j
                if live(m - 1, STEPS):
                    scores(m - 1)
                if live(m - 2, STEPS):
                    attend(m - 2, (j - 2) % 4, 4 * it + 2 * ((j - 2) // 2) + 2)
                if live(m, STEPS):
                    project(m, j, half, 2 * it + j // 2)
                if sides:
                    sides(m, 0)
                if live(m - 1, STEPS):
                    prob_T(m - 1)
                if live(m - 3, STEPS):
                    project_out(m - 3, (j - 3) % 4, 2 * it + (j - 3) // 2)

                if sides:
                    sides(m, 1)

            def first_norms(j, s):
                if s == 0 and j in (1, 2):
                    ln1_T(1 + j)

            def keys_T(pr):
                need(pe, xn_lo, 4)
                if pr < 3:
                    need(pe, lg_s, pr)
                else:
                    need(pe, uk_cp, pr)
                ln_transpose(0, 4 + pr, aux).then_inc(ln_T, 1)

            def outputs_T(pr):
                need(pe, y_s, pr + 1)
                bank_ = b_bank(pr)
                if pr < 2:
                    need(pe, uk_cp, pr + 1)
                elif pr == 2:
                    need(pe, pt_cp, STEPS)
                else:
                    need(pe, lg_s, pr)
                for b in range(2):
                    for ct in range(KT):
                        at = D * b + P * ct
                        mm = pe.transpose(bank_[:, at:at + P], uk[:, 2 * ct + b, :], ident[:])
                mm.then_inc(y_psum, 1)

            def x3_T(pr):
                need(pe, x2_s, pr + 1)
                ln_transpose(1, pr, b_bank(pr)).then_inc(x3_psum, 1)

            def gate_logits(pr):
                need(pe, x3_cp, pr + 1)
                for b in range(2):
                    for kt in range(KT):
                        at = C_GATE + NE * kt
                        mm = pe.matmul(b_bank(pr)[:, NE * b:NE * (b + 1)], x3f[:, kt, b * S:(b + 1) * S],
                                       cst[:, at:at + NE], start=kt == 0, stop=kt == KT - 1)
                mm.then_inc(lg_psum, 1)

            stages = {"keys_T": keys_T, "outputs_T": outputs_T, "x3_T": x3_T, "gate_logits": gate_logits}
            pe.wait_ge(idn, 5)
            pe.wait_ge(cst_in, 16)
            ln1_T(0)
            ln1_T(1)
            for j in range(4):
                step(0, j, 0, first_norms)
            with pe.Fori(1, 4) as it:
                for j in range(4):
                    step(it, j, 0)
            for j in range(4):
                step(4, j, 1)
            for m in range(20, STEPS + 3):
                step(m // 4, m % 4, 1, lambda m, s: beside_attention(stages, m, s))

            def up_projections(u, k, half):
                need(pe, w_lo, NH + u + 1)
                need(pe, x3_lo, 2 * (half + 1))
                xs = x3T[half]
                if isinstance(u, int) and u == 0:
                    for used in (q_lo, k_lo, v_cp, e_done):
                        pe.wait_ge(used, STEPS)
                for mt in range(2):
                    need(pe, h_s, 2 * u + mt - 1)
                    for mat, ps, ready in ((0, h1_ps, h1_psum), (1, hg_ps, hg_psum)):
                        split_mm(ps[mt][:], [([up(k, s, kt, mat, mt) for s in range(2)],
                                              [xs[s][:, kt, :] for s in range(2)])
                                             for kt in range(KT)]).then_inc(ready, 1)

            def down_projection(u, k):
                need(pe, h_lo, 2 * u + 2)
                need(pe, wo_lo, NH + u + 1)
                if isinstance(u, int) and u == 0:
                    pe.wait_ge(o_lo, STEPS)
                    pe.wait_ge(wo_add, STEPS)
                for bb in range(2):
                    need(pe, acc, 2 * u + bb - 1)
                    for i in range(2):
                        t = (2 * bb + i) * S
                        mm = split_mm(y_ps[bb][:, D * i:D * (i + 1)],
                                      [([o_s[s][:, 2 * k + kt, t:t + S] for s in range(2)],
                                        [wo_s[k][s][:, D * kt:D * (kt + 1)] for s in range(2)])
                                       for kt in range(KT)])
                    mm.then_inc(y2_psum, 1)

            for u in range(EXP):
                up_projections(u, u % 2, 0)
                beside_experts(stages, u, 0)
                if u:
                    down_projection(u - 1, (u - 1) % 2)
                beside_experts(stages, u, 1)
            beside_experts(stages, EXP, 0)
            up_projections(8, 0, 1)
            down_projection(7, 1)
            up_projections(9, 1, 1)
            down_projection(8, 0)
            with pe.Fori(5, 8) as t:
                for k in range(2):
                    u = 2 * t + k
                    up_projections(u, k, 1)
                    down_projection(u - 1, (k + 1) % 2)
            down_projection(15, 1)


def kernel(**inputs):
    import numpy as np
    import concourse.bacc as bacc
    from concourse import mybir as mb
    from concourse.bass_utils import run_bass_kernel_spmd

    a = {k: np.asarray(v) for k, v in inputs.items()}
    pairs = NH // 2

    def by_pair(mats, rows, tiles):
        t = np.stack(mats).reshape(len(mats), tiles, rows, pairs, 2 * DH)
        return np.ascontiguousarray(t.transpose(3, 2, 1, 0, 4)).reshape(pairs, rows, -1)

    def over_block(s):
        return s

    wqkv = by_pair([a[f"L0_attn_w{c}_codes"] for c in "qkv"], P, KT)
    sqkv = by_pair([a[f"L0_attn_w{c}_scales"] for c in "qkv"], P // BLK, KT)
    wo = a["L0_attn_wo_codes"].reshape(pairs, 2, P, D).transpose(0, 2, 1, 3).reshape(pairs, P, OW)
    so = a["L0_attn_wo_scales"].reshape(pairs, 2, P // BLK, D).transpose(0, 2, 1, 3).reshape(pairs, P // BLK, OW)
    w1 = np.concatenate([a["L0_ffn_W1"], a["L0_ffn_Ws1"][None]])
    wg = np.concatenate([a["L0_ffn_Wg"], a["L0_ffn_Wsg"][None]])
    w2 = np.concatenate([a["L0_ffn_W2"], a["L0_ffn_Ws2"][None]])
    wup = np.stack([w1, wg], 1).reshape(EXP, 2, KT, P, D).transpose(0, 3, 2, 1, 4).reshape(EXP, P, HW)
    wdown = w2.reshape(EXP, KT, P, D).transpose(0, 2, 1, 3).reshape(EXP, P, OW)
    cols = [a[f"L0_attn_b{c}"].reshape(NH, DH).T for c in "qkv"]
    cols += [a[f"L0_xattn_time_{c}"].reshape(KT, P).T for c in ("decay", "first")]
    cols += [a["L0_ffn_gate_w"].reshape(KT, P, NE).transpose(1, 0, 2).reshape(P, KT * NE)]
    rows = np.concatenate([a["L0_attn_bo"], a["L0_ffn_gate_b"], a["L0_ffn_biases"]])[None]
    arrays = {
        "x_in": a["x"].transpose(1, 0, 2),
        "ctx_in": a["ctx_2048"].reshape(NB * S, KT, P).transpose(2, 1, 0),
        "wqkv": wqkv, "sqkv": sqkv, "wo": wo, "so": so, "wup": wup, "wdown": wdown,
        "consts": np.concatenate(cols, 1), "rows": rows,
    }
    arrays = {k: np.ascontiguousarray(v) for k, v in arrays.items()}
    nc = bacc.Bacc("TRN2", target_bir_lowering=False, num_devices=1)
    t = {k: nc.dram_tensor(k, v.shape, mb.dt.from_np(v.dtype), kind="ExternalInput").ap()
         for k, v in arrays.items()}
    out = nc.dram_tensor("out", (S, NB, D), mb.dt.from_np(arrays["x_in"].dtype), kind="ExternalOutput").ap()
    decoder_layer(nc, t["x_in"], t["ctx_in"], t["wqkv"], t["sqkv"], t["wo"], t["so"], t["wup"], t["wdown"],
                  t["consts"], t["rows"], out)
    r = run_bass_kernel_spmd(nc, [arrays], core_ids=[0])
    return np.ascontiguousarray(r.results[0]["out"].transpose(1, 0, 2))
```

```python
from contextlib import ExitStack

import concourse.bass as bass
from concourse import mybir

F32 = mybir.dt.float32
F32R = mybir.dt.float32r
ALU = mybir.AluOpType
ACT = mybir.ActivationFunctionType
AX = mybir.AxisListType

P = 128
NB, S, D = 8, 128, 256
HALF = 4
T = HALF * S
NH, DH = 16, 128
KT = D // P
NE, TOPK = 7, 3
EXP = NE + 1
BLK = 32
STEPS = 2 * NH
UNITS = 2 * EXP
PW = KT * 3 * 2 * DH
OW = 2 * D
HW = KT * 2 * D
SEG = S + 1
EPS = 1e-5
EMPTY = -1e38
RESET = -2e38
SCALE = float(DH) ** -0.5

C_BQ, C_BK, C_BV, C_DECAY, C_FIRST, C_GATE = 0, NH, 2 * NH, 3 * NH, 3 * NH + KT, 3 * NH + 2 * KT
C_ALL = C_GATE + KT * NE
R_BO, R_GB, R_BIAS = 0, D, D + NE
R_ALL = D + 2 * NE
FIRST = 16 * (1 + P // BLK)
PASSES = ((0, 0), (0, 1), (1, 0))


def need(eng, sem, count):
    if not (isinstance(count, int) and count <= 0):
        eng.wait_ge(sem, count)


def live(i, n):
    return not isinstance(i, int) or 0 <= i < n


STAGES = {
    "stats_a": (0, -3), "norm_a": (2, 0), "keys_T": (2, 0), "k_copy": (3, 1),
    "uk_add": (3, 1), "maxima": (4, 2), "decayed": (4, 2), "exponents": (5, 2), "exponentials": (7, 4),
    "values": (7, 4), "scans": (8, 6), "outputs_1": (10, 8), "outputs_2": (11, 9), "outputs_T": (12, 10),
    "add_y": (13, 11), "norm_b": (14, 13), "x3_T": (14, 13), "x3_copies": (15, 14),
    "gate_logits": (15, 14), "x3_split": (15, 14), "logits": (16, 15),
}
EARLY = ("stats_a", "norm_a", "keys_T", "k_copy")
ATTENTION_AT = {0: (36, 36), 1: (40, 46)}
EXPERTS_AT = {2: (4, 4), 3: (8, 16)}
GATE_PARTS = (2, 7, 6)
GATE_STEPS = sum(GATE_PARTS)


def beside(table, clock, stages, now):
    for pr, starts in table.items():
        for name, stage in stages.items():
            if STAGES[name][clock] + starts[name not in EARLY] == now:
                stage(pr)


def beside_attention(stages, m, s):
    beside(ATTENTION_AT, 0, stages, 2 * m + s)


def beside_experts(stages, u, s):
    beside(EXPERTS_AT, 1, stages, 4 * u + s)


def decoder_layer(nc, x_in, ctx_in, wqkv, sqkv, wo, so, wup, wdown, consts, rows, out):
    with ExitStack() as stack:
        def sb(name, shape, dt=F32):
            return stack.enter_context(nc.sbuf_tensor(name, shape, dt))

        def bank(name):
            return stack.enter_context(nc.psum_tensor(name, [P, 512], F32))

        def sem(name):
            return stack.enter_context(nc.semaphore(name))

        x = sb("x", [P, NB, D])
        ctxT = sb("ctxT", [P, KT, NB * S])
        cst = sb("cst", [P, C_ALL])
        row = sb("row", [P, R_ALL])
        ident = sb("ident", [P, P])
        xnT = [[sb(f"xnT{h}{s}", [P, KT, T], F32R) for s in "hl"] for h in range(2)]
        x3T = [[sb(f"x3T{h}{s}", [P, KT, T], F32R) for s in "hl"] for h in range(2)]
        w_st = [sb(f"w_st{i}", [P, PW]) for i in range(2)]
        s_st = [sb(f"s_st{i}", [P, PW]) for i in range(2)]
        wo_st = [sb(f"wo_st{i}", [P, OW]) for i in range(2)]
        so_st = [sb(f"so_st{i}", [P, OW]) for i in range(2)]
        w_s = [[sb(f"w_s{i}{s}", [P, PW], F32R) for s in "hl"] for i in range(2)]
        wo_s = [[sb(f"wo_s{i}{s}", [P, OW], F32R) for s in "hl"] for i in range(2)]
        q_s = [sb(f"q{s}", [P, T], F32R) for s in "hl"]
        k_s = [sb(f"k{s}", [P, T], F32R) for s in "hl"]
        v_sb = [sb(f"v{i}", [P, HALF, 2 * DH]) for i in range(2)]
        e_sb = sb("e_sb", [P, HALF, S])
        pn = sb("pn", [P, HALF, S])
        pT = sb("pT", [P, HALF, S])
        o_s = [sb(f"o{s}", [P, 4, T], F32R) for s in "hl"]
        mx, nmx, rsum, rinv = (sb(n, [P, HALF]) for n in ("mx", "nmx", "rsum", "rinv"))
        st, mv, veps, rstd, lnx = [], [], [], [], []
        for i in range(2):
            st.append(sb(f"st{i}", [P, 2, 6]))
            mv.append(sb(f"mv{i}", [P, 2, 2]))
            veps.append(sb(f"veps{i}", [P, 2]))
            rstd.append(sb(f"rstd{i}", [P, 2]))
            lnx.append(sb(f"lnx{i}", [P, 2, D]))
        mhalf = sb("mhalf", [P, 2])
        segs = lambda name, n=1: sb(name, [P, n * KT * 2, SEG])
        decay, pp, ap, bp, vp = (segs(n) for n in ("decay", "pp", "ap", "bp", "vp"))
        kp = [segs(f"kp{i}") for i in range(2)]
        dd, ee = segs("dd", 4), segs("ee", 4)
        wneg = sb("wneg", [P, KT])
        uk, tq, num, den = (sb(n, [P, KT * 2, S]) for n in ("uk", "tq", "num", "den"))
        x3f = sb("x3f", [P, KT, 2 * S])
        lg = sb("lg", [P, NB, NE])
        g1, g2, gp, gb = (sb(n, [P, HALF, NE]) for n in ("g1", "g2", "gp", "gb"))
        gs = sb("gs", [P, HALF])
        gr = sb("gr", [P, HALF])
        tri = sb("tri", [P, NE, NE])
        r1, r2 = (sb(n, [P, HALF, NE, NE]) for n in ("r1", "r2"))
        we = sb("we", [P, NB, EXP])
        th = sb("th", [P, 2, T])
        hp = sb("hp", [P, 2, T])

        q_ps, k_ps, v_ps, s_ps, t_ps, o_ps, w_ps, aux = (
            bank(n) for n in ("q_ps", "k_ps", "v_ps", "s_ps", "t_ps", "o_ps", "w_ps", "aux"))
        h1_ps, hg_ps, y_ps = [q_ps, v_ps], [k_ps, s_ps], [o_ps, w_ps]

        x_in_s = [sem(f"x_in{i}") for i in range(3)]
        first_in, first_mul, first_hi, first_lo = (
            [sem(f"first_{n}{c}") for c in "qkv"] for n in ("in", "mul", "hi", "lo"))
        cst_in, row_in, ctx_in_s = sem("cst_in"), sem("row_in"), sem("ctx_in")
        w_in = [sem(f"w_in{i}") for i in range(2)]
        wo_in = [sem(f"wo_in{i}") for i in range(2)]
        stored = sem("stored")
        w_mul, w_hi, w_lo, wo_mul, wo_hi, wo_lo = (sem(n) for n in (
            "w_mul", "w_hi", "w_lo", "wo_mul", "wo_hi", "wo_lo"))
        q_psum, k_psum, v_psum, s_psum, t_psum, o_psum, wo_psum = (sem(n) for n in (
            "q_psum", "k_psum", "v_psum", "s_psum", "t_psum", "o_psum", "wo_psum"))
        q_hi, k_hi, q_lo, k_lo, v_cp, e_done, pt_cp, o_hi, o_lo = (sem(n) for n in (
            "q_hi", "k_hi", "q_lo", "k_lo", "v_cp", "e_done", "pt_cp", "o_hi", "o_lo"))
        s_max, n_max, r_inv, p_norm, wo_add = (sem(n) for n in (
            "s_max", "n_max", "r_inv", "p_norm", "wo_add"))
        ln_st, ln_mv, ln_ve, ln_rs, ln_x = ([sem(f"{n}_{a}") for a in "ab"] for n in (
            "ln_st", "ln_mv", "ln_ve", "ln_rs", "ln_x"))
        ln_T = sem("ln_T")
        xn_hi, xn_lo, x_bo = sem("xn_hi"), sem("xn_lo"), sem("x_bo")
        idn, consts_done, pads, wneg_s, dec_s = (sem(n) for n in (
            "idn", "consts_done", "pads", "wneg", "dec"))
        k_cp, uk_cp, p_scan, t_cp, q_max, d12_sub, d34_sub, e_exp, v_mul, a_scan, b_scan = (sem(n) for n in (
            "k_cp", "uk_cp", "p_scan", "t_cp", "q_max", "d12_sub", "d34_sub", "e_exp", "v_mul", "a_scan", "b_scan"))
        n1_s, n2_s, d1_s, num_s, den_s, rec_s, y_s, y_psum, x2_s = (sem(n) for n in (
            "n1", "n2", "d1", "num_s", "den_s", "rec_s", "y_s", "y_psum", "x2_s"))
        x3_psum, x3_cp, x3_hi, x3_lo, lg_psum, lg_s = (sem(n) for n in (
            "x3_psum", "x3_cp", "x3_hi", "x3_lo", "lg_psum", "lg_s"))
        g_step, g_exp, g_done = sem("g_step"), sem("g_exp"), sem("g_done")
        h1_psum, hg_psum, th_s, a_s, h_s, h_hi, h_lo, y2_psum, acc = (sem(n) for n in (
            "h1_psum", "hg_psum", "th_s", "a_s", "h_s", "h_hi", "h_lo", "y2_psum", "acc"))

        def qkv(i, s, kt, mat, a, b):
            at = (kt * 3 + mat) * 2 * DH
            return w_s[i][s][:, at + a:at + b]

        def matrix(t, mat):
            return t[:].rearrange("p (k m f) -> p k m f", k=KT, m=3)[:, :, mat, :]

        def up(i, s, kt, mat, mt):
            at = (kt * 2 + mat) * D + mt * P
            return w_s[i][s][:, at:at + P]

        def seg(t, i=0):
            return t[:, i * 2 * KT:(i + 1) * 2 * KT, 1:SEG]

        def before(t, i=0):
            return t[:, i * 2 * KT:(i + 1) * 2 * KT, 0:S]

        def flat(t, i=0):
            return t[:, i * 2 * KT:(i + 1) * 2 * KT, :].rearrange("p s t -> p (s t)")

        def b_bank(pr):
            return aux if pr < 2 else t_ps

        block = stack.enter_context(nc.Block())

        @block.sync
        def _(sp):
            def by_block(scales):
                rows_, n = scales.shape
                return scales.rearrange("b (o n) -> b o n", o=1).broadcast_to([rows_, BLK, n])

            def load_w(p, i, g):
                need(sp, w_lo, p - 2)
                sp.dma_start(w_st[i][:], wqkv[g]).then_inc(w_in[i], 16)
                sp.dma_start(s_st[i][:], by_block(sqkv[g])).then_inc(w_in[i], 16)

            def load_wo(p, i, g):
                need(sp, wo_lo, p - 1)
                sp.dma_start(wo_st[i][:], wo[g]).then_inc(wo_in[i], 16)
                sp.dma_start(so_st[i][:], by_block(so[g])).then_inc(wo_in[i], 16)

            def load_up(u, i, e):
                need(sp, w_lo, NH + u - 2)
                sp.dma_start(w_st[i][:, 0:HW], wup[e]).then_inc(w_in[i], 16)

            def load_down(u, i, e):
                need(sp, wo_lo, NH + u - 1)
                sp.dma_start(wo_st[i][:], wdown[e]).then_inc(wo_in[i], 16)

            sp.dma_start(x[:, 0:2, :], x_in[:, 0:2, :]).then_inc(x_in_s[0], 16)
            w0 = wqkv[0].rearrange("p (k m f) -> p k m f", k=KT, m=3)
            s0 = sqkv[0].rearrange("b (k m f) -> b k m f", k=KT, m=3)
            for mat in range(3):
                sp.dma_start(matrix(w_st[0], mat), w0[:, :, mat, :]).then_inc(first_in[mat], 16)
                for r in range(P // BLK):
                    sp.dma_start(matrix(s_st[0], mat)[r * BLK:(r + 1) * BLK],
                                 s0[r:r + 1, :, mat, :].broadcast_to([BLK, KT, 2 * DH])
                                 ).then_inc(first_in[mat], 16)
            load_wo(0, 0, 0)
            load_w(1, 1, 1)
            sp.dma_start(x[:, HALF:NB, :], x_in[:, HALF:NB, :]).then_inc(x_in_s[2], 16)
            for lo in first_lo:
                sp.wait_ge(lo, 1)
            for h in range(2):
                def two_pairs(t):
                    for k in range(2):
                        load_w(8 * h + 2 * t + 2 + k, k, 2 * t + 2 + k)
                        load_wo(8 * h + 2 * t + 1 + k, (1 + k) % 2, 2 * t + 1 + k)
                two_pairs(0)
                with sp.Fori(1, 3) as t:
                    two_pairs(t)
                if h == 0:
                    sp.dma_start(ctxT[:], ctx_in).then_inc(ctx_in_s, 16)
                    load_w(8, 0, 0)
                    load_wo(7, 1, 7)
                    load_w(9, 1, 1)
                    load_wo(8, 0, 0)
            load_up(0, 0, 0)
            load_wo(15, 1, 7)
            load_up(1, 1, 1)
            load_down(0, 0, 0)
            for h in range(2):
                with sp.Fori(0, 3) as t:
                    for k in range(2):
                        load_up(8 * h + 2 * t + 2 + k, k, 2 * t + 2 + k)
                        load_down(8 * h + 2 * t + 1 + k, (1 + k) % 2, 2 * t + 1 + k)
                if h == 0:
                    load_up(8, 0, 0)
                    load_down(7, 1, 7)
                    load_up(9, 1, 1)
                    load_down(8, 0, 0)
                else:
                    load_down(15, 1, 7)
            sp.wait_ge(acc, 2 * EXP)
            sp.dma_start(out[:, 0:HALF, :], x[:, 0:HALF, :]).then_inc(stored, 16)
            for bb in range(2):
                sp.wait_ge(acc, 4 * EXP - 1 + bb)
                b = HALF + 2 * bb
                sp.dma_start(out[:, b:b + 2, :], x[:, b:b + 2, :]).then_inc(stored, 16)
            sp.wait_ge(stored, 3 * 16)

        @block.gpsimd
        def _(pool):
            def mul_w(p, i, it):
                need(pool, w_in[i], 32 * (it + i))
                pool.tensor_tensor(w_st[i][:], w_st[i][:], s_st[i][:], ALU.mult).then_inc(w_mul, 1)

            def lo_w(p, i, n=PW):
                need(pool, w_hi, p)
                pool.tensor_tensor(w_s[i][1][:, 0:n], w_st[i][:, 0:n], w_s[i][0][:, 0:n].bitcast(F32),
                                   ALU.subtract).then_inc(w_lo, 1)

            def mul_wo(p, i, it):
                need(pool, wo_in[i], 32 * (it + 1))
                pool.tensor_tensor(wo_st[i][:], wo_st[i][:], so_st[i][:], ALU.mult).then_inc(wo_mul, 1)

            def lo_wo(p, i):
                need(pool, wo_hi, p + 1)
                pool.tensor_tensor(wo_s[i][1][:], wo_st[i][:], wo_s[i][0][:].bitcast(F32),
                                   ALU.subtract).then_inc(wo_lo, 1)

            def rstd_of(a, k):
                need(pool, ln_ve[a], k + 1)
                need(pool, ln_x[a], k)
                pool.tensor_tensor(rstd[a][:], veps[a][:], mhalf[:], ALU.pow).then_inc(ln_rs[a], 1)

            def add_bo(pr, b):
                need(pool, ln_x[0], pr + 1)
                if pr == 0:
                    pool.wait_ge(row_in, 16)
                bo = row[:, R_BO:R_BO + D].rearrange("p (o d) -> p o d", o=1).broadcast_to([P, 2, D])
                pool.tensor_tensor(x[:, b:b + 2, :], x[:, b:b + 2, :], bo, ALU.add).then_inc(x_bo, 1)

            def exponents(pr):
                need(pool, q_max, pr + 1)
                need(pool, t_cp, pr + 1)
                need(pool, e_exp, pr)
                pool.tensor_tensor(seg(dd, 2), tq[:], seg(pp), ALU.subtract)
                pool.tensor_tensor(seg(dd, 3), seg(kp[pr % 2]), seg(pp), ALU.subtract).then_inc(d34_sub, 1)

            def values(pr):
                b = 2 * pr
                if pr == 0:
                    pool.wait_ge(ctx_in_s, 16)
                need(pool, e_exp, pr + 1)
                for ct in range(KT):
                    v = ctxT[:, ct, b * S:(b + 2) * S].rearrange("p (b t) -> p b t", b=2)
                    i = pool.tensor_tensor(vp[:, 2 * ct:2 * ct + 2, 1:SEG],
                                           ee[:, 6 * KT + 2 * ct:6 * KT + 2 * ct + 2, 1:SEG], v, ALU.mult)
                i.then_inc(v_mul, 1)
                need(pool, y_s, pr)
                for ct in range(KT):
                    v = ctxT[:, ct, b * S:(b + 2) * S].rearrange("p (b t) -> p b t", b=2)
                    i = pool.tensor_tensor(num[:, 2 * ct:2 * ct + 2, :],
                                           ee[:, 2 * KT + 2 * ct:2 * KT + 2 * ct + 2, 1:SEG], v, ALU.mult)
                i.then_inc(n2_s, 1)
                need(pool, a_scan, pr + 1)
                pool.tensor_tensor(uk[:], seg(ee, 0), before(ap), ALU.mult).then_inc(n1_s, 1)
                need(pool, b_scan, pr + 1)
                need(pool, rec_s, 2 * pr)
                pool.tensor_tensor(den[:], seg(ee, 0), before(bp), ALU.mult).then_inc(d1_s, 1)

            def lo_x3(pr):
                h, c = pr // 2, 2 * S * (pr % 2)
                need(pool, x3_hi, pr + 1)
                pool.tensor_tensor(x3T[h][1][:, :, c:c + 2 * S], x3f[:],
                                   x3T[h][0][:, :, c:c + 2 * S].bitcast(F32),
                                   ALU.subtract).then_inc(x3_lo, 1)

            pool.memset(mhalf[:], -0.5).then_inc(idn, 1)
            pool.memset(ident[:], 0.0).then_inc(idn, 1)
            pool.memset(tri[:], 1.0).then_inc(idn, 1)
            pool.wait_ge(idn, 3)
            pool.affine_select(out=ident[:], in_=ident[:], compare_op=ALU.not_equal, fill=1.0, base=0,
                               pattern=[[-1, P]], channel_multiplier=1).then_inc(idn, 1)
            pool.affine_select(out=tri[:], in_=tri[:], compare_op=ALU.is_gt, fill=0.0, base=0,
                               pattern=[[1, NE], [-1, NE]], channel_multiplier=0).then_inc(idn, 1)
            rstd_of(0, 0)
            rstd_of(0, 1)
            pool.wait_ge(first_in[2], FIRST)
            v0 = matrix(w_st[0], 2)
            pool.tensor_tensor(v0, v0, matrix(s_st[0], 2), ALU.mult).then_inc(first_mul[2], 1)
            pool.wait_ge(first_hi[2], 1)
            pool.tensor_tensor(matrix(w_s[0][1], 2), v0, matrix(w_s[0][0], 2).bitcast(F32),
                               ALU.subtract).then_inc(first_lo[2], 1)
            mul_wo(0, 0, 0)
            mul_w(1, 1, 0)

            def turn(it, sides=None):
                for k in range(2):
                    p = 2 * it + 1 + k
                    lo_w(p, (1 + k) % 2, HW if isinstance(p, int) and p == NH else PW)
                    if sides:
                        sides(4 * it + 2 * k, 0)
                    if live(p + 1, NH):
                        mul_w(p + 1, k % 2, it + 1)
                    if sides:
                        sides(4 * it + 2 * k, 1)
                    lo_wo(p - 1, k)
                    if sides:
                        sides(4 * it + 2 * k + 1, 0)
                    if live(p, NH):
                        mul_wo(p, (1 + k) % 2, it + k)
                    if sides:
                        sides(4 * it + 2 * k + 1, 1)

            def first_norms(m, s):
                if m < 2 and s == 1:
                    add_bo(m, 2 * m)
                elif (m, s) == (1, 0):
                    rstd_of(0, 2)
                elif (m, s) == (2, 1):
                    rstd_of(0, 3)

            def half_1_bias(m, s):
                if m in (NH, NH + 1) and s == 1:
                    add_bo(2 + m - NH, HALF + 2 * (m - NH))

            stages = {
                "stats_a": lambda pr: rstd_of(0, 4 + pr), "exponents": exponents, "values": values,
                "add_y": lambda pr: rstd_of(1, pr), "x3_split": lo_x3,
            }
            turn(0, first_norms)
            with pool.Fori(1, 4) as it:
                turn(it)
            for t in range(4, 8):
                turn(t, lambda m, s: (half_1_bias(m, s), beside_attention(stages, m, s)))

            def unit(u, k, sides=None):
                if live(u + 1, UNITS):
                    lo_w(NH + u + 1, (k + 1) % 2, HW)
                if sides:
                    sides(u, 0)
                lo_wo(NH + u, k)
                if sides:
                    for s in range(1, 4):
                        sides(u, s)

            for u in range(EXP):
                unit(u, u % 2, lambda u, s: beside_experts(stages, u, s))
            unit(8, 0)
            unit(9, 1)
            with pool.Fori(5, 7) as t:
                for k in range(2):
                    unit(2 * t + k, k)
            unit(14, 0)
            unit(15, 1)

        @block.scalar
        def _(act):
            def ln1_hi(pr, h, hp_):
                need(act, ln_T, pr + 1)
                act.copy(xnT[h][0][:, :, 2 * S * hp_:2 * S * (hp_ + 1)],
                         aux[:].rearrange("p (k t) -> p k t", k=KT)).then_inc(xn_hi, 1)

            def softmax_exp(n):
                need(act, n_max, n + 1)
                need(act, p_norm, n)
                for b in range(HALF):
                    i = act.activation(e_sb[:, b, :], s_ps[:, b * S:(b + 1) * S], ACT.Exp, bias=nmx[:, b:b + 1],
                                       scale=SCALE, accum_out=rsum[:, b:b + 1])
                i.then_inc(e_done, 1)

            def hi_of(n, ps, dst, bias, ready, done, used):
                need(act, ready, n + 1)
                need(act, used, n)
                act.activation(dst, ps[:], ACT.Identity, bias=bias).then_inc(done, 1)

            def hi_w(p, i, n=PW):
                act.copy(w_s[i][0][:, 0:n], w_st[i][:, 0:n]).then_inc(w_hi, 1)

            def hi_wo(p, i):
                act.copy(wo_s[i][0][:], wo_st[i][:]).then_inc(wo_hi, 1)

            def k_copy(pr):
                need(act, ln_T, 4 + pr + 1)
                need(act, d34_sub, pr - 1)
                act.copy(seg(kp[pr % 2]), aux[:].rearrange("p (s t) -> p s t", t=S)).then_inc(k_cp, 1)

            def uk_add(pr):
                act.wait_ge(k_cp, pr + 1)
                need(act, y_psum, pr)
                for ct in range(KT):
                    i = act.activation(uk[:, 2 * ct:2 * ct + 2, :], kp[pr % 2][:, 2 * ct:2 * ct + 2, 1:SEG],
                                       ACT.Identity, bias=cst[:, C_FIRST + ct:C_FIRST + ct + 1])
                i.then_inc(uk_cp, 1)

            def decayed(pr):
                need(act, p_scan, pr + 1)
                if pr == 0:
                    act.wait_ge(dec_s, 1)
                for ct in range(KT):
                    i = act.activation(tq[:, 2 * ct:2 * ct + 2, :], pp[:, 2 * ct:2 * ct + 2, 0:S],
                                       ACT.Identity, bias=wneg[:, ct:ct + 1])
                i.then_inc(t_cp, 1)

            def exponentials(pr):
                need(act, d12_sub, pr + 1)
                need(act, d34_sub, pr + 1)
                act.activation(ee[:, :, 1:SEG], dd[:, :, 1:SEG], ACT.Exp).then_inc(e_exp, 1)

            def x3_copies(pr):
                h, c = pr // 2, 2 * S * (pr % 2)
                need(act, x3_psum, pr + 1)
                need(act, x3_lo, pr)
                act.copy(x3f[:], b_bank(pr)[:].rearrange("p (k t) -> p k t", k=KT)).then_inc(x3_cp, 1)
                act.wait_ge(x3_cp, pr + 1)
                act.copy(x3T[h][0][:, :, c:c + 2 * S], x3f[:]).then_inc(x3_hi, 1)

            act.dma_start(x[:, 2:HALF, :], x_in[:, 2:HALF, :]).then_inc(x_in_s[1], 16)
            act.dma_start(cst[:], consts).then_inc(cst_in, 16)
            act.dma_start(row[:], rows.broadcast_to([P, R_ALL])).then_inc(row_in, 16)
            for mat in range(3):
                act.wait_ge(first_mul[mat], 1)
                act.copy(matrix(w_s[0][0], mat), matrix(w_st[0], mat)).then_inc(first_hi[mat], 1)
                if mat < 2:
                    ln1_hi(mat, 0, mat)
            act.wait_ge(cst_in, 16)
            act.activation(wneg[:], cst[:, C_DECAY:C_DECAY + KT], ACT.Exp).then_inc(wneg_s, 1)

            def step(it, j, half, sides=None):
                m = 4 * it + j
                head = lambda i: i % NH if isinstance(i, int) else i - NH * half
                if live(m - 1, STEPS):
                    softmax_exp(m - 1)
                if live(m - 2, STEPS):
                    n = m - 2
                    hi_of(n, o_ps, o_s[0][:, (j - 2) % 4, :], cst[:, bass.ds(C_BV + head(n), 1)],
                          o_psum, o_hi, o_lo)
                if live(m, STEPS):
                    hi_of(m, q_ps, q_s[0][:], cst[:, bass.ds(C_BQ + head(m), 1)], q_psum, q_hi, q_lo)
                    hi_of(m, k_ps, k_s[0][:], cst[:, bass.ds(C_BK + head(m), 1)], k_psum, k_hi, k_lo)
                    need(act, v_psum, m + 1)
                    b = 2 * (j % 2)
                    act.copy(v_sb[j // 2 % 2][:, b:b + 2, :],
                             v_ps[:].rearrange("p (b f) -> p b f", b=2)).then_inc(v_cp, 1)
                if sides:
                    sides(0)
                if live(m - 1, STEPS):
                    need(act, t_psum, m)
                    act.copy(pT[:], t_ps[:].rearrange("p (b f) -> p b f", b=HALF)).then_inc(pt_cp, 1)
                if live(m, STEPS):
                    if j % 2:
                        p = 2 * it + (j + 3) // 2
                        if live(p, NH):
                            need(act, w_mul, p)
                            hi_w(p, (j + 3) // 2 % 2)
                    else:
                        p = 2 * it + j // 2
                        need(act, wo_mul, p + 1)
                        need(act, wo_psum, 2 * p - 2)
                        hi_wo(p, j // 2 % 2)
                if sides:
                    sides(1)

            def turn(it, half, sides=None):
                for j in range(4):
                    step(it, j, half, (lambda s: sides(j, s)) if sides else None)

            def first_norms(j, s):
                if (j, s) == (0, 1):
                    act.wait_ge(w_mul, 1)
                    hi_w(1, 1)
                elif s == 0 and j >= 2:
                    ln1_hi(j, 1, j - 2)

            stages = {"k_copy": k_copy, "uk_add": uk_add, "decayed": decayed, "exponentials": exponentials,
                      "x3_copies": x3_copies}
            turn(0, 0, first_norms)
            with act.Fori(1, 4) as it:
                turn(it, 0)

            def loaded(t, i):
                return 32 * (NH // 2 - 1 + i) + 16 * (t + 1)

            for m in range(NH, STEPS + 2):
                if m == STEPS - 2:
                    act.wait_ge(v_psum, STEPS - 2)
                    act.wait_ge(w_in[0], loaded(0, 0))
                    hi_w(NH, 0, HW)
                step(m // 4, m % 4, 1, lambda s: beside_attention(stages, m, s))
                if m == STEPS:
                    act.wait_ge(v_psum, STEPS)
                    act.wait_ge(w_in[1], loaded(0, 1))
                    hi_w(NH + 1, 1, HW)

            def gate_exp(h):
                act.wait_ge(g_step, GATE_STEPS * h + GATE_PARTS[0])
                act.activation(gp[:], g1[:], ACT.Exp).then_inc(g_exp, 1)

            def unit(t, k, sides=None):
                u, n = 2 * t + k, (k + 1) % 2
                if live(u + 1, UNITS) and not (isinstance(u, int) and u == 0):
                    act.wait_ge(w_in[n], loaded(t + k, n))
                    need(act, hg_psum, 2 * u)
                    hi_w(NH + u + 1, n, HW)
                act.wait_ge(wo_in[k], loaded(t, 1))
                if isinstance(u, int) and u < 2:
                    act.wait_ge(wo_psum, STEPS - 2 + 2 * u)
                need(act, y2_psum, 2 * u - 2)
                hi_wo(NH + u, k)
                if sides:
                    sides(0)
                for mt in range(2):
                    r = 2 * u + mt
                    need(act, h1_psum, r + 1)
                    need(act, h_s, r - 1)
                    act.activation(th[:, mt, :], h1_ps[mt][:], ACT.Tanh, scale=0.5).then_inc(th_s, 1)
                    if sides and mt == 0:
                        sides(1)
                    need(act, h_s, r + 1)
                    if isinstance(u, int) and u < 2:
                        act.wait_ge(wo_psum, STEPS)
                    act.copy(o_s[0][:, 2 * k + mt, :], hp[:, mt, :]).then_inc(h_hi, 1)
                    if sides:
                        sides(2 + mt)

            def gate_or_beside(u, s):
                if u % EXP == 0 and s == 1:
                    gate_exp(u // EXP)
                if u < EXP:
                    beside_experts(stages, u, s)

            for u in range(EXP + 2):
                unit(u // 2, u % 2, lambda s: gate_or_beside(u, s))
            with act.Fori(5, 7) as t:
                for k in range(2):
                    unit(t, k)
            unit(7, 0)
            unit(7, 1)

        @block.vector
        def _(dve):
            sub, mult, add = ALU.subtract, ALU.mult, ALU.add

            def stats(a, k, b):
                need(dve, ln_mv[a], k)
                for i in range(2):
                    s = dve.bn_stats(st[a][:, i, :], x[:, b + i, :])
                s.then_inc(ln_st[a], 1)
                dve.wait_ge(ln_st[a], k + 1)
                need(dve, ln_x[a], k)
                for i in range(2):
                    s = dve.bn_aggr(mv[a][:, i, :], st[a][:, i, :])
                s.then_inc(ln_mv[a], 1)
                dve.wait_ge(ln_mv[a], k + 1)
                need(dve, ln_rs[a], k)
                dve.tensor_scalar(veps[a][:], mv[a][:, :, 1], EPS, None, add).then_inc(ln_ve[a], 1)

            def normalised(a, k, b):
                need(dve, ln_rs[a], k + 1)
                need(dve, x3_psum if a else ln_T, k)
                for i in range(2):
                    s = dve.tensor_scalar(lnx[a][:, i, :], x[:, b + i, :], mv[a][:, i, 0:1],
                                          rstd[a][:, i:i + 1], sub, mult)
                s.then_inc(ln_x[a], 1)

            def ln1_lo(pr, h, hp_):
                need(dve, xn_hi, pr + 1)
                c = slice(2 * S * hp_, 2 * S * (hp_ + 1))
                dve.tensor_tensor(xnT[h][1][:, :, c], aux[:].rearrange("p (k t) -> p k t", k=KT),
                                  xnT[h][0][:, :, c].bitcast(F32), sub).then_inc(xn_lo, 1)

            def add_out(w, j, half):
                need(dve, wo_psum, w + 1)
                if isinstance(w, int):
                    half = w // NH
                    if w < 2:
                        dve.wait_ge(x_bo, w + 1)
                    elif NH <= w < NH + 2:
                        dve.wait_ge(x_bo, w - NH + 3)
                need(dve, wo_add, w)
                b = HALF * half + 2 * (j % 2)
                xb = x[:, b:b + 2, :]
                dve.tensor_tensor(xb, w_ps[:].rearrange("p (b d) -> p b d", b=2), xb, add).then_inc(wo_add, 1)

            def softmax_max(n):
                need(dve, s_psum, n + 1)
                need(dve, n_max, n)
                dve.tensor_reduce(mx[:], s_ps[:].rearrange("p (b k) -> p b k", b=HALF), AX.X,
                                  ALU.max).then_inc(s_max, 1)
                dve.wait_ge(s_max, n + 1)
                need(dve, e_done, n)
                dve.tensor_scalar(nmx[:], mx[:], -SCALE, None, mult).then_inc(n_max, 1)

            def softmax_norm(n):
                need(dve, e_done, n + 1)
                need(dve, p_norm, n)
                dve.reciprocal(rinv[:], rsum[:]).then_inc(r_inv, 1)
                dve.wait_ge(r_inv, n + 1)
                need(dve, t_psum, n)
                ri = rinv[:].rearrange("p (b o) -> p b o", o=1).broadcast_to([P, HALF, S])
                dve.tensor_tensor(pn[:], e_sb[:], ri, mult).then_inc(p_norm, 1)

            def lo_of(n, ps, hi, lo, bias, ready, done):
                need(dve, ready, n + 1)
                dve.scalar_tensor_tensor(lo, ps[:], bias, hi.bitcast(F32), add, sub).then_inc(done, 1)

            def maxima(pr):
                need(dve, uk_cp, pr + 1)
                if pr == 0:
                    dve.wait_ge(pads, 1)
                dve.tensor_tensor_scan(flat(pp), flat(decay), flat(kp[pr % 2]), 0.0, add, ALU.max).then_inc(p_scan, 1)
                dve.wait_ge(p_scan, pr + 1)
                need(dve, n1_s, pr)
                dve.tensor_tensor(seg(ap), before(pp), uk[:], ALU.max).then_inc(q_max, 1)
                dve.wait_ge(q_max, pr + 1)
                need(dve, e_exp, pr)
                dve.tensor_tensor(seg(dd, 0), before(pp), seg(ap), sub)
                dve.tensor_tensor(seg(dd, 1), uk[:], seg(ap), sub).then_inc(d12_sub, 1)

            def scans(pr):
                need(dve, v_mul, pr + 1)
                dve.tensor_tensor_scan(flat(ap), flat(ee, 2), flat(vp), 0.0, mult, add).then_inc(a_scan, 1)
                dve.tensor_tensor_scan(flat(bp), flat(ee, 2), flat(ee, 3), 0.0, mult, add).then_inc(b_scan, 1)

            def outputs_1(pr):
                need(dve, n1_s, pr + 1)
                dve.tensor_tensor(num[:], num[:], uk[:], add).then_inc(num_s, 1)
                need(dve, d1_s, pr + 1)
                dve.tensor_tensor(den[:], den[:], seg(ee, 1), add).then_inc(den_s, 1)
                dve.wait_ge(den_s, pr + 1)
                dve.reciprocal(tq[:, 0:2, :], den[:, 0:2, :]).then_inc(rec_s, 1)

            def outputs_2(pr):
                dve.reciprocal(tq[:, 2:4, :], den[:, 2:4, :]).then_inc(rec_s, 1)
                dve.wait_ge(rec_s, 2 * pr + 2)
                need(dve, y_psum, pr)
                dve.tensor_tensor(uk[:], num[:], tq[:], mult).then_inc(y_s, 1)

            def add_y(pr):
                b = 2 * pr
                need(dve, y_psum, pr + 1)
                for i in range(2):
                    s = dve.tensor_tensor(x[:, b + i, :], b_bank(pr)[:, D * i:D * (i + 1)], x[:, b + i, :], add)
                s.then_inc(x2_s, 1)
                dve.wait_ge(x2_s, pr + 1)
                stats(1, pr, b)

            def logits(pr):
                b = 2 * pr
                need(dve, lg_psum, pr + 1)
                for i in range(2):
                    s = dve.tensor_tensor(lg[:, b + i, :], b_bank(pr)[:, NE * i:NE * (i + 1)], row[:, R_GB:R_GB + NE],
                                          add)
                s.then_inc(lg_s, 1)

            def first_mul_of(mat):
                dve.wait_ge(first_in[mat], FIRST)
                w0 = matrix(w_st[0], mat)
                dve.tensor_tensor(w0, w0, matrix(s_st[0], mat), mult).then_inc(first_mul[mat], 1)

            def first_lo_of(mat):
                dve.wait_ge(first_hi[mat], 1)
                dve.tensor_tensor(matrix(w_s[0][1], mat), matrix(w_st[0], mat),
                                  matrix(w_s[0][0], mat).bitcast(F32), sub).then_inc(first_lo[mat], 1)

            dve.wait_ge(x_in_s[0], 16)
            stats(0, 0, 0)
            first_mul_of(0)
            normalised(0, 0, 0)
            dve.wait_ge(x_in_s[1], 16)
            stats(0, 1, 2)
            first_lo_of(0)
            first_mul_of(1)
            normalised(0, 1, 2)
            ln1_lo(0, 0, 0)
            first_lo_of(1)
            ln1_lo(1, 0, 1)

            def recurrence_constants():
                for t, v in ((kp[0], EMPTY), (kp[1], EMPTY), (vp, 0.0), (ee, 0.0)):
                    dve.memset(t[:, :, 0], v).then_inc(consts_done, 1)
                dve.memset(we[:], 1.0).then_inc(consts_done, 1)
                dve.memset(decay[:], 0.0).then_inc(consts_done, 1)
                dve.wait_ge(wneg_s, 1)
                dve.tensor_scalar(wneg[:], wneg[:], -1.0, None, mult).then_inc(dec_s, 1)
                dve.wait_ge(dec_s, 1)
                dve.wait_ge(consts_done, 6)
                for ct in range(KT):
                    c = decay[:, 2 * ct:2 * ct + 2, 1:SEG]
                    dve.tensor_scalar(c, c, wneg[:, ct:ct + 1], None, add)
                dve.memset(decay[:, :, 0], RESET).then_inc(pads, 1)

            def step(it, j, half, sides=None):
                m = 4 * it + j
                head = lambda i: i % NH if isinstance(i, int) else i - NH * half
                if live(m - 1, STEPS):
                    softmax_max(m - 1)
                if live(m - 4, STEPS):
                    add_out(m - 4, j, half)
                if live(m - 1, STEPS):
                    softmax_norm(m - 1)
                if sides:
                    sides(m, 0)
                if live(m - 2, STEPS):
                    n, i = m - 2, (j - 2) % 4
                    lo_of(n, o_ps, o_s[0][:, i, :], o_s[1][:, i, :], cst[:, bass.ds(C_BV + head(n), 1)],
                          o_hi, o_lo)
                if live(m, STEPS):
                    lo_of(m, q_ps, q_s[0][:], q_s[1][:], cst[:, bass.ds(C_BQ + head(m), 1)], q_hi, q_lo)
                    lo_of(m, k_ps, k_s[0][:], k_s[1][:], cst[:, bass.ds(C_BK + head(m), 1)], k_hi, k_lo)
                if sides:
                    sides(m, 1)

            def first_norms(j, s):
                if (j, s) == (1, 0):
                    dve.wait_ge(x_in_s[2], 16)
                    stats(0, 2, HALF)
                elif s == 0 and j >= 2:
                    normalised(0, j, HALF + 2 * (j - 2))
                elif s == 1 and j >= 2:
                    if j == 2:
                        stats(0, 3, HALF + 2)
                    ln1_lo(j, 1, j - 2)

            def stats_a(pr):
                dve.wait_ge(wo_add, NH * (pr // 2 + 1) - 1 + pr % 2)
                stats(0, 4 + pr, 2 * pr)

            stages = {
                "stats_a": stats_a, "norm_a": lambda pr: normalised(0, 4 + pr, 2 * pr), "maxima": maxima,
                "scans": scans, "outputs_1": outputs_1, "outputs_2": outputs_2, "add_y": add_y,
                "norm_b": lambda pr: normalised(1, pr, 2 * pr), "logits": logits,
            }
            for j in range(4):
                step(0, j, 0, first_norms)
            with dve.Fori(1, 4) as it:
                for j in range(4):
                    step(it, j, 0)
            for m in range(NH, STEPS + 4):
                step(m // 4, m % 4, 1, lambda m, s: beside_attention(stages, m, s))
                if m == NH:
                    recurrence_constants()

            def gate(h, part):
                c = slice(HALF * h, HALF * (h + 1))
                cast = lambda t: t.rearrange("p (b o) -> p b o", o=1).broadcast_to([P, HALF, NE])
                count = [GATE_STEPS * h + sum(GATE_PARTS[:part])]

                def then(i):
                    count[0] += 1
                    i.then_inc(g_step, 1)
                    dve.wait_ge(g_step, count[0])

                if part == 0:
                    dve.wait_ge(lg_s, 2 * (h + 1))
                    then(dve.tensor_reduce(gs[:], lg[:, c, :], AX.X, ALU.max))
                    then(dve.tensor_tensor(g1[:], lg[:, c, :], cast(gs[:]), sub))
                elif part == 1:
                    dve.wait_ge(g_exp, h + 1)
                    then(dve.tensor_reduce(gs[:], gp[:], AX.X, add))
                    then(dve.reciprocal(gr[:], gs[:]))
                    then(dve.tensor_tensor(g2[:], gp[:], cast(gr[:]), mult))
                    bias = row[:, R_BIAS:R_BIAS + NE].rearrange("p (o e) -> p o e", o=1).broadcast_to([P, HALF, NE])
                    then(dve.tensor_tensor(gb[:], g2[:], bias, add))
                    other = gb[:].rearrange("p b (o j) -> p b o j", o=1).broadcast_to([P, HALF, NE, NE])
                    own = gb[:].rearrange("p b (e o) -> p b e o", o=1).broadcast_to([P, HALF, NE, NE])
                    before_ = tri[:].rearrange("p (o e) j -> p o e j", o=1).broadcast_to([P, HALF, NE, NE])
                    then(dve.tensor_tensor(r1[:], other, own, ALU.is_gt))
                    then(dve.tensor_tensor(r2[:], other, own, ALU.is_equal))
                    then(dve.tensor_tensor(r2[:], r2[:], before_, mult))
                else:
                    then(dve.tensor_tensor(r1[:], r1[:], r2[:], add))
                    then(dve.tensor_reduce(g1[:], r1[:], AX.X, add))
                    then(dve.scalar_tensor_tensor(g1[:], g1[:], float(TOPK), g2[:], ALU.is_lt, mult))
                    then(dve.tensor_reduce(gs[:], g1[:], AX.X, add))
                    then(dve.reciprocal(gr[:], gs[:]))
                    dve.wait_ge(consts_done, 6)
                    then(dve.tensor_tensor(we[:, c, 0:NE], g1[:], cast(gr[:]), mult))

            def add_expert(u, half):
                for bb in range(2):
                    need(dve, y2_psum, 2 * u + bb + 1)
                    need(dve, acc, 2 * u + bb - 1)
                    for i in range(2):
                        b = HALF * half + 2 * bb + i
                        e = u - EXP * half
                        s = dve.scalar_tensor_tensor(x[:, b, :], y_ps[bb][:, D * i:D * (i + 1)],
                                                     we[:, b, bass.ds(e, 1)], x[:, b, :], mult, add)
                    s.then_inc(acc, 1)

            def lo_h(u, k):
                for mt in range(2):
                    need(dve, h_hi, 2 * u + mt + 1)
                    dve.tensor_tensor(o_s[1][:, 2 * k + mt, :], hp[:, mt, :],
                                      o_s[0][:, 2 * k + mt, :].bitcast(F32), sub).then_inc(h_lo, 1)

            def unit(t, k, half, sides=None):
                u = 2 * t + k
                if live(u - 1, UNITS):
                    lo_h(u - 1, (k + 1) % 2)
                if sides:
                    sides(u, 0)
                if live(u - 2, UNITS):
                    add_expert(u - 2, (u - 2) // EXP if isinstance(u, int) else half)
                if sides:
                    sides(u, 1)
                for mt in range(2):
                    r = 2 * u + mt
                    need(dve, th_s, r + 1)
                    dve.scalar_tensor_tensor(th[:, mt, :], th[:, mt, :], 1.0, h1_ps[mt][:], add,
                                             mult).then_inc(a_s, 1)
                    dve.wait_ge(a_s, r + 1)
                    need(dve, hg_psum, r + 1)
                    need(dve, h_lo, r - 1)
                    dve.scalar_tensor_tensor(hp[:, mt, :], th[:, mt, :], 0.5, hg_ps[mt][:], mult,
                                             mult).then_inc(h_s, 1)
                    if sides:
                        sides(u, 2 + mt)

            def gate_or_beside(u, s):
                if u % EXP == 0 and s != 1:
                    gate(u // EXP, (0, None, 1, 2)[s])
                if u < EXP:
                    beside_experts(stages, u, s)

            for u in range(EXP + 2):
                unit(u // 2, u % 2, u // EXP, gate_or_beside)
            with dve.Fori(5, 7) as t:
                for k in range(2):
                    unit(t, k, 1)
            unit(7, 0, 1)
            unit(7, 1, 1)
            lo_h(15, 1)
            add_expert(14, 1)
            add_expert(15, 1)

        @block.tensor
        def _(pe):
            def split_mm(out_, pairs):
                every = [(l[a], r[b]) for l, r in pairs for a, b in PASSES]
                for i, (l, r) in enumerate(every):
                    mm = pe.matmul(out_, l, r, start=i == 0, stop=i == len(every) - 1)
                return mm

            def ln_transpose(a, k, bank_):
                need(pe, ln_x[a], k + 1)
                for kt in range(KT):
                    for b in range(2):
                        at = (2 * kt + b) * S
                        mm = pe.transpose(bank_[:, at:at + S], lnx[a][:, b, kt * P:(kt + 1) * P], ident[:])
                return mm

            def ln1_T(pr):
                need(pe, xn_lo, pr)
                ln_transpose(0, pr, aux).then_inc(ln_T, 1)

            def scores(n):
                need(pe, q_lo, n + 1)
                need(pe, k_lo, n + 1)
                need(pe, e_done, n)
                for b in range(HALF):
                    c = slice(b * S, (b + 1) * S)
                    mm = split_mm(s_ps[:, c], [([t[:, c] for t in q_s], [t[:, c] for t in k_s])])
                mm.then_inc(s_psum, 1)

            def attend(n, j, vcount):
                need(pe, pt_cp, n + 1)
                need(pe, v_cp, vcount)
                need(pe, o_lo, n)
                i, f = j // 2, (j % 2) * DH
                for b in range(HALF):
                    mm = pe.matmul(o_ps[:, b * S:(b + 1) * S], v_sb[i][:, b, f:f + DH], pT[:, b, :],
                                   start=True, stop=True)
                mm.then_inc(o_psum, 1)

            def project(m, j, half, pair):
                i, f = j // 2, (j % 2) * DH
                xs = xnT[half]
                if not (isinstance(pair, int) and pair == 0):
                    need(pe, w_lo, pair)
                need(pe, xn_lo, 2 * (half + 1))
                for mat, ps, ready, used in ((0, q_ps, q_psum, q_lo), (1, k_ps, k_psum, k_lo)):
                    if isinstance(m, int) and m == 0:
                        pe.wait_ge(first_lo[mat], 1)
                    need(pe, used, m)
                    split_mm(ps[:], [([qkv(i, s, kt, mat, f, f + DH) for s in range(2)],
                                      [xs[s][:, kt, :] for s in range(2)]) for kt in range(KT)]).then_inc(ready, 1)
                need(pe, v_cp, m)
                if isinstance(m, int) and m == 0:
                    pe.wait_ge(first_lo[2], 1)
                for b in range(2):
                    t = (2 * (j % 2) + b) * S
                    mm = split_mm(v_ps[:, 2 * DH * b:2 * DH * (b + 1)],
                                  [([xs[s][:, kt, t:t + S] for s in range(2)],
                                    [qkv(i, s, kt, 2, 0, 2 * DH) for s in range(2)]) for kt in range(KT)])
                mm.then_inc(v_psum, 1)

            def prob_T(n):
                need(pe, p_norm, n + 1)
                need(pe, pt_cp, n)
                for b in range(HALF):
                    mm = pe.transpose(t_ps[:, b * S:(b + 1) * S], pn[:, b, :], ident[:])
                mm.then_inc(t_psum, 1)

            def project_out(w, j, pair):
                need(pe, o_lo, 2 * pair + 2)
                need(pe, wo_lo, pair + 1)
                need(pe, wo_add, w)
                i = j // 2
                for b in range(2):
                    t = (2 * (j % 2) + b) * S
                    mm = split_mm(w_ps[:, D * b:D * (b + 1)],
                                  [([o_s[s][:, 2 * i + h, t:t + S] for s in range(2)],
                                    [wo_s[i][s][:, D * h:D * (h + 1)] for s in range(2)]) for h in range(2)])
                mm.then_inc(wo_psum, 1)

            def step(it, j, half, sides=None, filler=None):
                m = 4 * it + j
                if live(m - 1, STEPS):
                    scores(m - 1)
                if filler and not live(m - 1, STEPS):
                    filler()
                if live(m - 2, STEPS):
                    attend(m - 2, (j - 2) % 4, 4 * it + 2 * ((j - 2) // 2) + 2)
                if filler and live(m - 1, STEPS):
                    filler()
                if live(m, STEPS):
                    project(m, j, half, 2 * it + j // 2)
                if sides:
                    sides(m, 0)
                if live(m - 1, STEPS):
                    prob_T(m - 1)
                if live(m - 3, STEPS):
                    project_out(m - 3, (j - 3) % 4, 2 * it + (j - 3) // 2)
                if sides:
                    sides(m, 1)

            def first_norms(j, s):
                if s == 0 and j >= 2:
                    ln1_T(j)

            def keys_T(pr):
                need(pe, xn_lo, 4)
                need(pe, k_cp, pr)
                if pr == 2:
                    pe.wait_ge(lg_s, 2)
                ln_transpose(0, 4 + pr, aux).then_inc(ln_T, 1)

            def outputs_T(pr):
                need(pe, y_s, pr + 1)
                bank_ = b_bank(pr)
                if pr == 0:
                    pe.wait_ge(k_cp, 2)
                elif pr == 2:
                    pe.wait_ge(pt_cp, STEPS)
                else:
                    pe.wait_ge(lg_s, pr)
                for b in range(2):
                    for ct in range(KT):
                        at = D * b + P * ct
                        mm = pe.transpose(bank_[:, at:at + P], uk[:, 2 * ct + b, :], ident[:])
                mm.then_inc(y_psum, 1)

            def x3_T(pr):
                need(pe, x2_s, pr + 1)
                ln_transpose(1, pr, b_bank(pr)).then_inc(x3_psum, 1)

            def gate_logits(pr):
                need(pe, x3_cp, pr + 1)
                for b in range(2):
                    for kt in range(KT):
                        at = C_GATE + NE * kt
                        mm = pe.matmul(b_bank(pr)[:, NE * b:NE * (b + 1)], x3f[:, kt, b * S:(b + 1) * S],
                                       cst[:, at:at + NE], start=kt == 0, stop=kt == KT - 1)
                mm.then_inc(lg_psum, 1)

            stages = {"keys_T": keys_T, "outputs_T": outputs_T, "x3_T": x3_T, "gate_logits": gate_logits}
            pe.wait_ge(idn, 5)
            pe.wait_ge(cst_in, 16)
            ln1_T(0)
            ln1_T(1)
            for j in range(4):
                step(0, j, 0, first_norms)
            with pe.Fori(1, 4) as it:
                for j in range(4):
                    step(it, j, 0)

            def up_projection(u, k, half, mt):
                need(pe, w_lo, NH + u)
                need(pe, x3_lo, 2 * (half + 1))
                xs = x3T[half]
                if isinstance(u, int) and u == 0:
                    for used in ((q_lo, k_lo), (v_cp, e_done))[mt]:
                        pe.wait_ge(used, STEPS)
                need(pe, h_s, 2 * u + mt - 1)
                for mat, ps, ready in ((0, h1_ps, h1_psum), (1, hg_ps, hg_psum)):
                    split_mm(ps[mt][:], [([up(k, s, kt, mat, mt) for s in range(2)],
                                          [xs[s][:, kt, :] for s in range(2)])
                                         for kt in range(KT)]).then_inc(ready, 1)

            def down_projection(u, k, bb):
                need(pe, h_lo, 2 * u + 2)
                need(pe, wo_lo, NH + u + 1)
                if isinstance(u, int) and u == 0:
                    pe.wait_ge(o_lo, STEPS)
                    pe.wait_ge(wo_add, STEPS)
                need(pe, acc, 2 * u + bb - 1)
                for i in range(2):
                    t = (2 * bb + i) * S
                    mm = split_mm(y_ps[bb][:, D * i:D * (i + 1)],
                                  [([o_s[s][:, 2 * k + kt, t:t + S] for s in range(2)],
                                    [wo_s[k][s][:, D * kt:D * (kt + 1)] for s in range(2)])
                                   for kt in range(KT)])
                mm.then_inc(y2_psum, 1)

            for m in range(NH, STEPS + 3):
                step(m // 4, m % 4, 1, lambda m, s: beside_attention(stages, m, s),
                     (lambda: up_projection(0, 0, 0, m - STEPS)) if STEPS <= m < STEPS + 2 else None)
            for s in range(4):
                beside_experts(stages, 0, s)
            for u in range(1, EXP + 2):
                for i in range(4):
                    if i < 2:
                        up_projection(u, u % 2, u // EXP, i)
                    else:
                        down_projection(u - 1, (u - 1) % 2, i - 2)
                    if u < EXP:
                        beside_experts(stages, u, i)
            with pe.Fori(5, 8) as t:
                for k in range(2):
                    u = 2 * t + k
                    for mt in range(2):
                        up_projection(u, k, 1, mt)
                    for bb in range(2):
                        down_projection(u - 1, (k + 1) % 2, bb)
            for bb in range(2):
                down_projection(15, 1, bb)


def kernel(**inputs):
    import numpy as np
    import concourse.bacc as bacc
    from concourse import mybir as mb
    from concourse.bass_utils import run_bass_kernel_spmd

    a = {k: np.asarray(v) for k, v in inputs.items()}
    pairs = NH // 2

    def by_pair(mats, rows, tiles):
        t = np.stack(mats).reshape(len(mats), tiles, rows, pairs, 2 * DH)
        return np.ascontiguousarray(t.transpose(3, 2, 1, 0, 4)).reshape(pairs, rows, -1)

    def over_block(s):
        return s

    wqkv = by_pair([a[f"L0_attn_w{c}_codes"] for c in "qkv"], P, KT)
    sqkv = by_pair([a[f"L0_attn_w{c}_scales"] for c in "qkv"], P // BLK, KT)
    wo = a["L0_attn_wo_codes"].reshape(pairs, 2, P, D).transpose(0, 2, 1, 3).reshape(pairs, P, OW)
    so = a["L0_attn_wo_scales"].reshape(pairs, 2, P // BLK, D).transpose(0, 2, 1, 3).reshape(pairs, P // BLK, OW)
    w1 = np.concatenate([a["L0_ffn_W1"], a["L0_ffn_Ws1"][None]])
    wg = np.concatenate([a["L0_ffn_Wg"], a["L0_ffn_Wsg"][None]])
    w2 = np.concatenate([a["L0_ffn_W2"], a["L0_ffn_Ws2"][None]])
    wup = np.stack([w1, wg], 1).reshape(EXP, 2, KT, P, D).transpose(0, 3, 2, 1, 4).reshape(EXP, P, HW)
    wdown = w2.reshape(EXP, KT, P, D).transpose(0, 2, 1, 3).reshape(EXP, P, OW)
    cols = [a[f"L0_attn_b{c}"].reshape(NH, DH).T for c in "qkv"]
    cols += [a[f"L0_xattn_time_{c}"].reshape(KT, P).T for c in ("decay", "first")]
    cols += [a["L0_ffn_gate_w"].reshape(KT, P, NE).transpose(1, 0, 2).reshape(P, KT * NE)]
    rows = np.concatenate([a["L0_attn_bo"], a["L0_ffn_gate_b"], a["L0_ffn_biases"]])[None]
    arrays = {
        "x_in": a["x"].transpose(1, 0, 2),
        "ctx_in": a["ctx_2048"].reshape(NB * S, KT, P).transpose(2, 1, 0),
        "wqkv": wqkv, "sqkv": sqkv, "wo": wo, "so": so, "wup": wup, "wdown": wdown,
        "consts": np.concatenate(cols, 1), "rows": rows,
    }
    arrays = {k: np.ascontiguousarray(v) for k, v in arrays.items()}
    nc = bacc.Bacc("TRN2", target_bir_lowering=False, num_devices=1)
    t = {k: nc.dram_tensor(k, v.shape, mb.dt.from_np(v.dtype), kind="ExternalInput").ap()
         for k, v in arrays.items()}
    out = nc.dram_tensor("out", (S, NB, D), mb.dt.from_np(arrays["x_in"].dtype), kind="ExternalOutput").ap()
    decoder_layer(nc, t["x_in"], t["ctx_in"], t["wqkv"], t["sqkv"], t["wo"], t["so"], t["wup"], t["wdown"],
                  t["consts"], t["rows"], out)
    r = run_bass_kernel_spmd(nc, [arrays], core_ids=[0])
    return np.ascontiguousarray(r.results[0]["out"].transpose(1, 0, 2))
```

```python
from contextlib import ExitStack

import concourse.bass as bass
from concourse import mybir

F32 = mybir.dt.float32
F32R = mybir.dt.float32r
ALU = mybir.AluOpType
ACT = mybir.ActivationFunctionType
AX = mybir.AxisListType

P = 128
NB, S, D = 8, 128, 256
HALF = 4
T = HALF * S
NH, DH = 16, 128
KT = D // P
NE, TOPK = 7, 3
EXP = NE + 1
BLK = 32
STEPS = 2 * NH
UNITS = 2 * EXP
PW = KT * 3 * 2 * DH
OW = 2 * D
HW = KT * 2 * D
SEG = S + 1
EPS = 1e-5
EMPTY = -1e38
RESET = -2e38
SCALE = float(DH) ** -0.5

C_BQ, C_BK, C_BV, C_DECAY, C_FIRST, C_GATE = 0, NH, 2 * NH, 3 * NH, 3 * NH + KT, 3 * NH + 2 * KT
C_ALL = C_GATE + KT * NE
R_BO, R_GB, R_BIAS = 0, D, D + NE
R_ALL = D + 2 * NE
PASSES = ((0, 0), (0, 1), (1, 0))


def need(eng, sem, count):
    if not (isinstance(count, int) and count <= 0):
        eng.wait_ge(sem, count)


def live(i, n):
    return not isinstance(i, int) or 0 <= i < n


STAGES = {
    "stats_a": (1, -3), "norm_a": (2, -1), "keys_T": (2, 0), "k_copy": (2, 1),
    "uk_add": (3, 1), "maxima": (5, 2), "decayed": (5, 2), "exponents": (5, 2), "exp_12": (6, 5),
    "exp_34": (7, 5), "value_products": (7, 5), "scans": (9, 7), "state_products": (9, 7), "sums": (10, 10),
    "inverse_1": (11, 11), "inverse_2": (13, 12), "outputs_T": (14, 13), "add_y": (15, 13), "norm_b": (16, 15),
    "x3_T": (16, 16), "x3_copies": (17, 17), "gate_logits": (18, 18), "x3_split": (17, 17), "logits": (19, 19),
}
EARLY = ("stats_a", "norm_a", "keys_T", "k_copy")
ATTENTION_AT = {0: (36, 36), 1: (40, 44)}
EXPERTS_AT = {2: (8, 8), 3: (12, 14)}
GATE_PARTS = (2, 7, 6)
GATE_STEPS = sum(GATE_PARTS)


def beside(table, clock, stages, now):
    for pr, starts in table.items():
        for name, stage in stages.items():
            if STAGES[name][clock] + starts[name not in EARLY] == now:
                stage(pr)


def beside_attention(stages, m, s):
    beside(ATTENTION_AT, 0, stages, 2 * m + s)


def beside_experts(stages, u, s):
    beside(EXPERTS_AT, 1, stages, 4 * u + s)


def decoder_layer(nc, x_in, ctx_in, wqkv, sqkv, wo, so, wup, wdown, consts, rows, out):
    with ExitStack() as stack:
        def sb(name, shape, dt=F32):
            return stack.enter_context(nc.sbuf_tensor(name, shape, dt))

        def bank(name):
            return stack.enter_context(nc.psum_tensor(name, [P, 512], F32))

        def sem(name):
            return stack.enter_context(nc.semaphore(name))

        x = sb("x", [P, NB, D])
        ctxT = sb("ctxT", [P, KT, NB * S])
        cst = sb("cst", [P, C_ALL])
        row = sb("row", [P, R_ALL])
        ident = sb("ident", [P, P])
        xnT = [[sb(f"xnT{h}{s}", [P, KT, T], F32R) for s in "hl"] for h in range(2)]
        x3T = [[sb(f"x3T{h}{s}", [P, KT, T], F32R) for s in "hl"] for h in range(2)]
        w_st = [sb(f"w_st{i}", [P, PW]) for i in range(2)]
        s_st = [sb(f"s_st{i}", [P, PW]) for i in range(2)]
        wo_st = [sb(f"wo_st{i}", [P, OW]) for i in range(2)]
        so_st = [sb(f"so_st{i}", [P, OW]) for i in range(2)]
        w_s = [[sb(f"w_s{i}{s}", [P, PW], F32R) for s in "hl"] for i in range(2)]
        wo_s = [[sb(f"wo_s{i}{s}", [P, OW], F32R) for s in "hl"] for i in range(2)]
        q_sb, k_sb = sb("q_sb", [P, T]), sb("k_sb", [P, T])
        v_sb = [sb(f"v{i}", [P, HALF, 2 * DH]) for i in range(2)]
        e_sb = sb("e_sb", [P, HALF, S])
        pn = sb("pn", [P, HALF, S])
        pT = sb("pT", [P, HALF, S])
        o_s = [sb(f"o{s}", [P, 4, T], F32R) for s in "hl"]
        mx, nmx, rsum, rinv = (sb(n, [P, HALF]) for n in ("mx", "nmx", "rsum", "rinv"))
        st, mv, veps, rstd, lnx = [], [], [], [], []
        for i in range(2):
            st.append(sb(f"st{i}", [P, 2, 6]))
            mv.append(sb(f"mv{i}", [P, 2, 2]))
            veps.append(sb(f"veps{i}", [P, 2]))
            rstd.append(sb(f"rstd{i}", [P, 2]))
            lnx.append(sb(f"lnx{i}", [P, 2, D]))
        mhalf = sb("mhalf", [P, 2])
        segs = lambda name, n=1: sb(name, [P, n * KT * 2, SEG])
        decay, pp, ap, bp, vp = (segs(n) for n in ("decay", "pp", "ap", "bp", "vp"))
        kp = [segs(f"kp{i}") for i in range(2)]
        dd, ee = segs("dd", 4), segs("ee", 4)
        wneg = sb("wneg", [P, KT])
        uk, tq, num, den = (sb(n, [P, KT * 2, S]) for n in ("uk", "tq", "num", "den"))
        uk = [uk] * 3 + [e_sb]
        x3f = sb("x3f", [P, KT, 2 * S])
        lg = sb("lg", [P, NB, NE])
        g1, g2, gp, gb = (sb(n, [P, HALF, NE]) for n in ("g1", "g2", "gp", "gb"))
        gs = sb("gs", [P, HALF])
        gr = sb("gr", [P, HALF])
        tri = sb("tri", [P, NE, NE])
        r1, r2 = (sb(n, [P, HALF, NE, NE]) for n in ("r1", "r2"))
        we = sb("we", [P, NB, EXP])
        sl = sb("sl", [P, 2, T])
        hp = sb("hp", [P, 2, T])

        q_ps, k_ps, v_ps, s_ps, t_ps, o_ps, w_ps, aux = (
            bank(n) for n in ("q_ps", "k_ps", "v_ps", "s_ps", "t_ps", "o_ps", "w_ps", "aux"))
        h1_ps, hg_ps, y_ps = [q_ps, v_ps], [k_ps, s_ps], [o_ps, w_ps]

        x_in_s = [sem(f"x_in{i}") for i in range(3)]
        first_in, first_mul, first_hi, first_lo = (
            [sem(f"first_{n}{c}") for c in "qkv"] for n in ("in", "mul", "hi", "lo"))
        cst_in, row_in, ctx_in_s = sem("cst_in"), sem("row_in"), sem("ctx_in")
        w_in = [sem(f"w_in{i}") for i in range(2)]
        wo_in = [sem(f"wo_in{i}") for i in range(2)]
        stored = sem("stored")
        w_mul, w_hi, w_lo, wo_mul, wo_hi, wo_lo = (sem(n) for n in (
            "w_mul", "w_hi", "w_lo", "wo_mul", "wo_hi", "wo_lo"))
        q_psum, k_psum, v_psum, s_psum, t_psum, o_psum, wo_psum = (sem(n) for n in (
            "q_psum", "k_psum", "v_psum", "s_psum", "t_psum", "o_psum", "wo_psum"))
        q_done, k_done, v_cp, e_done, pt_cp, o_hi, o_lo = (sem(n) for n in (
            "q_done", "k_done", "v_cp", "e_done", "pt_cp", "o_hi", "o_lo"))
        s_max, n_max, r_inv, p_norm, wo_add = (sem(n) for n in (
            "s_max", "n_max", "r_inv", "p_norm", "wo_add"))
        ln_st, ln_mv, ln_ve, ln_rs, ln_x = ([sem(f"{n}_{a}") for a in "ab"] for n in (
            "ln_st", "ln_mv", "ln_ve", "ln_rs", "ln_x"))
        ln_T = sem("ln_T")
        xn_hi, xn_lo, x_bo = sem("xn_hi"), sem("xn_lo"), sem("x_bo")
        idn, consts_done, pads, wneg_s, dec_s = (sem(n) for n in (
            "idn", "consts_done", "pads", "wneg", "dec"))
        k_cp, uk_cp, p_scan, t_cp, q_max, d12_sub, d34_sub, e12_exp, e34_exp, v_mul, a_scan, b_scan = (sem(n) for n in (
            "k_cp", "uk_cp", "p_scan", "t_cp", "q_max", "d12_sub", "d34_sub", "e12_exp", "e34_exp", "v_mul", "a_scan", "b_scan"))
        n1_s, n2_s, d1_s, num_s, den_s, rec_s, y_s, y_psum, x2_s = (sem(n) for n in (
            "n1", "n2", "d1", "num_s", "den_s", "rec_s", "y_s", "y_psum", "x2_s"))
        x3_psum, x3_cp, x3_hi, x3_lo, lg_psum, lg_s = (sem(n) for n in (
            "x3_psum", "x3_cp", "x3_hi", "x3_lo", "lg_psum", "lg_s"))
        g_step, g_exp, g_done = sem("g_step"), sem("g_exp"), sem("g_done")
        h1_psum, hg_psum, sl_s, h_s, h_hi, y2_psum, acc = (sem(n) for n in (
            "h1_psum", "hg_psum", "sl_s", "h_s", "h_hi", "y2_psum", "acc"))
        h_lo = [sem(f"h_lo{mt}") for mt in range(2)]

        def qkv(i, s, kt, mat, a, b):
            at = (mat * KT + kt) * 2 * DH
            return w_s[i][s][:, at + a:at + b]

        def by_block(scales):
            rows_, n = scales.shape
            return scales.rearrange("b (o n) -> b o n", o=1).broadcast_to([rows_, BLK, n])

        def matrix(t, mat):
            return t[:, mat * PW // 3:(mat + 1) * PW // 3]

        def up(i, s, kt, mat, mt):
            at = (kt * 2 + mat) * D + mt * P
            return w_s[i][s][:, at:at + P]

        def seg(t, i=0):
            return t[:, i * 2 * KT:(i + 1) * 2 * KT, 1:SEG]

        def before(t, i=0):
            return t[:, i * 2 * KT:(i + 1) * 2 * KT, 0:S]

        def flat(t, i=0):
            return t[:, i * 2 * KT:(i + 1) * 2 * KT, :].rearrange("p s t -> p (s t)")

        def b_bank(pr):
            return aux if pr < 2 else t_ps

        block = stack.enter_context(nc.Block())

        @block.sync
        def _(sp):
            def load_w(p, i, g):
                need(sp, w_lo, p - 2)
                sp.dma_start(w_st[i][:], wqkv[g]).then_inc(w_in[i], 16)
                sp.dma_start(s_st[i][:], by_block(sqkv[g])).then_inc(w_in[i], 16)

            def load_wo(p, i, g):
                need(sp, wo_lo, p - 1)
                sp.dma_start(wo_st[i][:], wo[g]).then_inc(wo_in[i], 16)
                sp.dma_start(so_st[i][:], by_block(so[g])).then_inc(wo_in[i], 16)

            def load_up(u, i, e):
                need(sp, w_lo, NH + u - 2)
                sp.dma_start(w_st[i][:, 0:HW], wup[e]).then_inc(w_in[i], 16)

            def load_down(u, i, e):
                need(sp, wo_lo, NH + u - 1)
                sp.dma_start(wo_st[i][:], wdown[e]).then_inc(wo_in[i], 16)

            sp.dma_start(x[:, 0:2, :], x_in[:, 0:2, :]).then_inc(x_in_s[0], 16)
            for mat in range(3):
                sp.dma_start(matrix(w_st[0], mat), matrix(wqkv[0], mat)).then_inc(first_in[mat], 16)
                if mat:
                    sp.dma_start(matrix(s_st[0], mat), by_block(matrix(sqkv[0], mat))).then_inc(first_in[mat], 16)
            load_wo(0, 0, 0)
            load_w(1, 1, 1)
            sp.dma_start(x[:, HALF:NB, :], x_in[:, HALF:NB, :]).then_inc(x_in_s[2], 16)
            for lo in first_lo:
                sp.wait_ge(lo, 1)
            for h in range(2):
                def two_pairs(t):
                    for k in range(2):
                        load_w(8 * h + 2 * t + 2 + k, k, 2 * t + 2 + k)
                        load_wo(8 * h + 2 * t + 1 + k, (1 + k) % 2, 2 * t + 1 + k)
                two_pairs(0)
                with sp.Fori(1, 3) as t:
                    two_pairs(t)
                if h == 0:
                    sp.dma_start(ctxT[:], ctx_in).then_inc(ctx_in_s, 16)
                    load_w(8, 0, 0)
                    load_wo(7, 1, 7)
                    load_w(9, 1, 1)
                    load_wo(8, 0, 0)
            load_up(0, 0, 0)
            load_wo(15, 1, 7)
            load_up(1, 1, 1)
            load_down(0, 0, 0)
            for h in range(2):
                with sp.Fori(0, 3) as t:
                    for k in range(2):
                        load_up(8 * h + 2 * t + 2 + k, k, 2 * t + 2 + k)
                        load_down(8 * h + 2 * t + 1 + k, (1 + k) % 2, 2 * t + 1 + k)
                if h == 0:
                    load_up(8, 0, 0)
                    load_down(7, 1, 7)
                    load_up(9, 1, 1)
                    load_down(8, 0, 0)
                else:
                    load_down(15, 1, 7)
            sp.wait_ge(acc, 2 * EXP)
            sp.dma_start(out[:, 0:HALF, :], x[:, 0:HALF, :]).then_inc(stored, 16)
            for bb in range(2):
                sp.wait_ge(acc, 4 * EXP - 1 + bb)
                b = HALF + 2 * bb
                sp.dma_start(out[:, b:b + 2, :], x[:, b:b + 2, :]).then_inc(stored, 16)
            sp.wait_ge(stored, 3 * 16)

        @block.gpsimd
        def _(pool):
            def mul_w(p, i, it):
                need(pool, w_in[i], 32 * (it + i))
                pool.tensor_tensor(w_st[i][:], w_st[i][:], s_st[i][:], ALU.mult).then_inc(w_mul, 1)

            def lo_w(p, i, n=PW):
                need(pool, w_hi, p)
                pool.tensor_tensor(w_s[i][1][:, 0:n], w_st[i][:, 0:n], w_s[i][0][:, 0:n].bitcast(F32),
                                   ALU.subtract).then_inc(w_lo, 1)

            def mul_wo(p, i, it):
                need(pool, wo_in[i], 32 * (it + 1))
                pool.tensor_tensor(wo_st[i][:], wo_st[i][:], so_st[i][:], ALU.mult).then_inc(wo_mul, 1)

            def lo_down(u, i):
                need(pool, wo_hi, NH + u + 1)
                pool.tensor_tensor(wo_s[i][1][:], wo_st[i][:], wo_s[i][0][:].bitcast(F32),
                                   ALU.subtract).then_inc(wo_lo, 1)

            def rstd_of(a, k):
                need(pool, ln_ve[a], k + 1)
                need(pool, ln_x[a], k)
                pool.tensor_tensor(rstd[a][:], veps[a][:], mhalf[:], ALU.pow).then_inc(ln_rs[a], 1)

            def add_bo(pr, b):
                need(pool, ln_x[0], pr + 1)
                if pr == 0:
                    pool.wait_ge(row_in, 16)
                bo = row[:, R_BO:R_BO + D].rearrange("p (o d) -> p o d", o=1).broadcast_to([P, 2, D])
                pool.tensor_tensor(x[:, b:b + 2, :], x[:, b:b + 2, :], bo, ALU.add).then_inc(x_bo, 1)

            def exponents(pr):
                need(pool, q_max, pr + 1)
                need(pool, t_cp, pr + 1)
                need(pool, e34_exp, pr)
                pool.tensor_tensor(seg(dd, 2), seg(dd, 2), seg(pp), ALU.subtract)
                pool.tensor_tensor(seg(dd, 3), seg(kp[pr % 2]), seg(pp), ALU.subtract).then_inc(d34_sub, 1)

            def value_products(pr):
                b = 2 * pr
                if pr == 0:
                    pool.wait_ge(ctx_in_s, 16)
                need(pool, e12_exp, pr + 1)
                need(pool, y_psum, pr)
                for ct in range(KT):
                    v = ctxT[:, ct, b * S:(b + 2) * S].rearrange("p (b t) -> p b t", b=2)
                    i = pool.tensor_tensor(num[:, 2 * ct:2 * ct + 2, :],
                                           ee[:, 2 * KT + 2 * ct:2 * KT + 2 * ct + 2, 1:SEG], v, ALU.mult)
                i.then_inc(n2_s, 1)

            def state_products(pr):
                need(pool, a_scan, pr + 1)
                pool.tensor_tensor(uk[pr][:], seg(ee, 0), before(ap), ALU.mult).then_inc(n1_s, 1)
                need(pool, b_scan, pr + 1)
                need(pool, rec_s, 2 * pr)
                pool.tensor_tensor(den[:], seg(ee, 0), before(bp), ALU.mult).then_inc(d1_s, 1)

            def lo_x3(pr):
                h, c = pr // 2, 2 * S * (pr % 2)
                need(pool, x3_hi, pr + 1)
                pool.tensor_tensor(x3T[h][1][:, :, c:c + 2 * S], x3f[:],
                                   x3T[h][0][:, :, c:c + 2 * S].bitcast(F32),
                                   ALU.subtract).then_inc(x3_lo, 1)

            pool.memset(mhalf[:], -0.5).then_inc(idn, 1)
            pool.memset(ident[:], 0.0).then_inc(idn, 1)
            pool.memset(tri[:], 1.0).then_inc(idn, 1)
            pool.wait_ge(idn, 3)
            pool.affine_select(out=ident[:], in_=ident[:], compare_op=ALU.not_equal, fill=1.0, base=0,
                               pattern=[[-1, P]], channel_multiplier=1).then_inc(idn, 1)
            pool.affine_select(out=tri[:], in_=tri[:], compare_op=ALU.is_gt, fill=0.0, base=0,
                               pattern=[[1, NE], [-1, NE]], channel_multiplier=0).then_inc(idn, 1)
            rstd_of(0, 0)
            rstd_of(0, 1)
            pool.wait_ge(first_in[2], 32)
            v0 = matrix(w_st[0], 2)
            pool.tensor_tensor(v0, v0, matrix(s_st[0], 2), ALU.mult).then_inc(first_mul[2], 1)
            pool.wait_ge(first_hi[2], 1)
            pool.tensor_tensor(matrix(w_s[0][1], 2), v0, matrix(w_s[0][0], 2).bitcast(F32),
                               ALU.subtract).then_inc(first_lo[2], 1)
            mul_wo(0, 0, 0)
            mul_w(1, 1, 0)

            def turn(it, sides=None):
                for k in range(2):
                    p = 2 * it + 1 + k
                    if isinstance(p, int) and p > NH // 2:
                        if p < NH:
                            if p == NH // 2 + 1:
                                pool.wait_ge(w_lo, NH // 2)
                            lo_w(p, (1 + k) % 2)
                        if sides:
                            sides(4 * it + 2 * k, 0)
                            sides(4 * it + 2 * k, 1)
                        if live(p + 1, NH):
                            mul_w(p + 1, k % 2, it + 1)
                    else:
                        mul_w(p + 1, k % 2, it + 1)
                        if sides:
                            sides(4 * it + 2 * k, 0)
                            sides(4 * it + 2 * k, 1)
                    if live(p, NH):
                        mul_wo(p, (1 + k) % 2, it + k)
                    if sides:
                        sides(4 * it + 2 * k + 1, 0)
                        sides(4 * it + 2 * k + 1, 1)

            def first_norms(m, s):
                if (m, s) == (1, 0):
                    rstd_of(0, 2)
                elif (m, s) == (2, 1):
                    rstd_of(0, 3)
                elif s == 1 and m % 2:
                    add_bo(m // 2, 2 * (m // 2))

            def half_1_bias(m, s):
                if m in (NH, NH + 1) and s == 1:
                    add_bo(2 + m - NH, HALF + 2 * (m - NH))

            stages = {
                "stats_a": lambda pr: rstd_of(0, 4 + pr), "exponents": exponents, "value_products": value_products,
                "state_products": state_products,
                "add_y": lambda pr: rstd_of(1, pr), "x3_split": lo_x3,
            }
            turn(0, first_norms)
            with pool.Fori(1, 4) as it:
                turn(it)
            for t in range(4, 8):
                turn(t, lambda m, s: (half_1_bias(m, s), beside_attention(stages, m, s)))

            lo_w(NH, 0, HW)
            pool.wait_ge(wo_lo, NH)

            def lo_h(u, k):
                need(pool, h_hi, 2 * u + 2)
                pool.tensor_tensor(o_s[1][:, 2 * k + 1, :], hp[:, 1, :], o_s[0][:, 2 * k + 1, :].bitcast(F32),
                                   ALU.subtract).then_inc(h_lo[1], 1)

            def unit(u, k, sides=None):
                if live(u - 1, UNITS):
                    lo_h(u - 1, 1 - k)
                if live(u + 1, UNITS):
                    lo_w(NH + u + 1, (k + 1) % 2, HW)
                if sides:
                    sides(u, 0)
                lo_down(u, k)
                if sides:
                    for s in range(1, 4):
                        sides(u, s)

            for u in range(EXP + 2):
                unit(u, u % 2, lambda u, s: beside_experts(stages, u, s))
            with pool.Fori(5, 7) as t:
                for k in range(2):
                    unit(2 * t + k, k)
            unit(14, 0)
            unit(15, 1)
            lo_h(15, 1)

        @block.scalar
        def _(act):
            def ln1_hi(pr, h, hp_):
                need(act, ln_T, pr + 1)
                act.copy(xnT[h][0][:, :, 2 * S * hp_:2 * S * (hp_ + 1)],
                         aux[:].rearrange("p (k t) -> p k t", k=KT)).then_inc(xn_hi, 1)

            def softmax_exp(n):
                need(act, n_max, n + 1)
                need(act, p_norm, n)
                for b in range(HALF):
                    i = act.activation(e_sb[:, b, :], s_ps[:, b * S:(b + 1) * S], ACT.Exp, bias=nmx[:, b:b + 1],
                                       scale=SCALE, accum_out=rsum[:, b:b + 1])
                i.then_inc(e_done, 1)

            def biased(n, ps, dst, bias, ready, done, used):
                need(act, ready, n + 1)
                need(act, used, n)
                act.activation(dst, ps[:], ACT.Identity, bias=bias).then_inc(done, 1)

            def hi_w(p, i, n=PW):
                act.copy(w_s[i][0][:, 0:n], w_st[i][:, 0:n]).then_inc(w_hi, 1)

            def hi_wo(p, i):
                act.copy(wo_s[i][0][:], wo_st[i][:]).then_inc(wo_hi, 1)

            def k_copy(pr):
                need(act, ln_T, 4 + pr + 1)
                need(act, d34_sub, pr - 1)
                act.copy(seg(kp[pr % 2]), aux[:].rearrange("p (s t) -> p s t", t=S)).then_inc(k_cp, 1)

            def uk_add(pr):
                act.wait_ge(k_cp, pr + 1)
                if pr < 3:
                    need(act, num_s, pr)
                for ct in range(KT):
                    i = act.activation(uk[pr][:, 2 * ct:2 * ct + 2, :], kp[pr % 2][:, 2 * ct:2 * ct + 2, 1:SEG],
                                       ACT.Identity, bias=cst[:, C_FIRST + ct:C_FIRST + ct + 1])
                i.then_inc(uk_cp, 1)

            def decayed(pr):
                need(act, p_scan, pr + 1)
                if pr == 0:
                    act.wait_ge(dec_s, 1)
                need(act, e34_exp, pr)
                for ct in range(KT):
                    at = 4 * KT + 2 * ct
                    i = act.activation(dd[:, at:at + 2, 1:SEG], pp[:, 2 * ct:2 * ct + 2, 0:S],
                                       ACT.Identity, bias=wneg[:, ct:ct + 1])
                i.then_inc(t_cp, 1)

            def exp_12(pr):
                need(act, d12_sub, pr + 1)
                need(act, den_s, pr)
                act.activation(ee[:, 0:4 * KT, 1:SEG], dd[:, 0:4 * KT, 1:SEG], ACT.Exp).then_inc(e12_exp, 1)

            def exp_34(pr):
                need(act, d34_sub, pr + 1)
                need(act, b_scan, pr)
                act.activation(ee[:, 4 * KT:, 1:SEG], dd[:, 4 * KT:, 1:SEG], ACT.Exp).then_inc(e34_exp, 1)

            def x3_copies(pr):
                h, c = pr // 2, 2 * S * (pr % 2)
                need(act, x3_psum, pr + 1)
                need(act, x3_lo, pr)
                act.copy(x3f[:], b_bank(pr)[:].rearrange("p (k t) -> p k t", k=KT)).then_inc(x3_cp, 1)
                act.wait_ge(x3_cp, pr + 1)
                act.copy(x3T[h][0][:, :, c:c + 2 * S], x3f[:]).then_inc(x3_hi, 1)

            act.dma_start(matrix(s_st[0], 0), by_block(matrix(sqkv[0], 0))).then_inc(first_in[0], 16)
            act.dma_start(x[:, 2:HALF, :], x_in[:, 2:HALF, :]).then_inc(x_in_s[1], 16)
            act.dma_start(cst[:], consts).then_inc(cst_in, 16)
            act.dma_start(row[:], rows.broadcast_to([P, R_ALL])).then_inc(row_in, 16)
            for mat in range(3):
                act.wait_ge(first_mul[mat], 1)
                act.copy(matrix(w_s[0][0], mat), matrix(w_st[0], mat)).then_inc(first_hi[mat], 1)
                if mat < 2:
                    ln1_hi(mat, 0, mat)
            act.wait_ge(cst_in, 16)
            act.activation(wneg[:], cst[:, C_DECAY:C_DECAY + KT], ACT.Exp).then_inc(wneg_s, 1)

            def step(it, j, half, sides=None):
                m = 4 * it + j
                head = lambda i: i % NH if isinstance(i, int) else i - NH * half
                if live(m - 1, STEPS):
                    softmax_exp(m - 1)
                if live(m - 2, STEPS):
                    n = m - 2
                    biased(n, o_ps, o_s[0][:, (j - 2) % 4, :], cst[:, bass.ds(C_BV + head(n), 1)],
                          o_psum, o_hi, o_lo)
                if live(m, STEPS):
                    biased(m, q_ps, q_sb[:], cst[:, bass.ds(C_BQ + head(m), 1)], q_psum, q_done, s_psum)
                    need(act, v_psum, m + 1)
                    b = 2 * (j % 2)
                    act.copy(v_sb[j // 2 % 2][:, b:b + 2, :],
                             v_ps[:].rearrange("p (b f) -> p b f", b=2)).then_inc(v_cp, 1)
                if sides:
                    sides(0)
                if live(m - 1, STEPS):
                    need(act, t_psum, m)
                    act.copy(pT[:], t_ps[:].rearrange("p (b f) -> p b f", b=HALF)).then_inc(pt_cp, 1)
                if live(m, STEPS):
                    if j % 2:
                        p = 2 * it + (j + 3) // 2
                        if live(p, NH):
                            need(act, w_mul, p)
                            hi_w(p, (j + 3) // 2 % 2)
                    else:
                        p = 2 * it + j // 2
                        need(act, wo_mul, p + 1)
                        need(act, wo_psum, 2 * p - 2)
                        hi_wo(p, j // 2 % 2)
                        if isinstance(m, int) and m == 0:
                            act.wait_ge(w_mul, 1)
                            hi_w(1, 1)
                if sides:
                    sides(1)

            def turn(it, half, sides=None):
                for j in range(4):
                    step(it, j, half, (lambda s: sides(j, s)) if sides else None)

            def first_norms(j, s):
                if s == 0 and j >= 2:
                    ln1_hi(j, 1, j - 2)

            stages = {"k_copy": k_copy, "uk_add": uk_add, "decayed": decayed, "exp_12": exp_12, "exp_34": exp_34,
                      "x3_copies": x3_copies}
            turn(0, 0, first_norms)
            with act.Fori(1, 4) as it:
                turn(it, 0)

            def loaded(t, i):
                return 32 * (NH // 2 - 1 + i) + 16 * (t + 1)

            def gate_exp(h):
                act.wait_ge(g_step, GATE_STEPS * h + GATE_PARTS[0])
                act.activation(gp[:], g1[:], ACT.Exp).then_inc(g_exp, 1)

            def silu(r, mt):
                need(act, h1_psum, r + 1)
                need(act, h_s, r - 1)
                act.activation(sl[:, mt, :], h1_ps[mt][:], ACT.Silu).then_inc(sl_s, 1)

            for m in range(NH, STEPS + 2):
                if m == STEPS - 2:
                    act.wait_ge(v_psum, STEPS - 2)
                    act.wait_ge(w_in[0], loaded(0, 0))
                    hi_w(NH, 0, HW)
                step(m // 4, m % 4, 1, lambda s: beside_attention(stages, m, s))
                if m == STEPS:
                    act.wait_ge(v_psum, STEPS)
                    act.wait_ge(w_in[1], loaded(0, 1))
                    hi_w(NH + 1, 1, HW)
                    gate_exp(0)
                    for mt in range(2):
                        silu(mt, mt)

            def unit(t, k, sides=None):
                u, n = 2 * t + k, (k + 1) % 2
                if live(u + 1, UNITS) and not (isinstance(u, int) and u == 0):
                    act.wait_ge(w_in[n], loaded(t + k, n))
                    need(act, hg_psum, 2 * u)
                    hi_w(NH + u + 1, n, HW)
                act.wait_ge(wo_in[k], loaded(t, 1))
                if isinstance(u, int) and u < 2:
                    act.wait_ge(wo_psum, STEPS - 2 + 2 * u)
                need(act, y2_psum, 2 * u - 2)
                hi_wo(NH + u, k)
                if sides:
                    sides(0)
                for mt in range(2):
                    r = 2 * u + mt
                    if not (isinstance(u, int) and u == 0):
                        silu(r, mt)
                    if sides and mt == 0:
                        sides(1)
                    need(act, h_s, r + 1)
                    act.copy(o_s[0][:, 2 * k + mt, :], hp[:, mt, :]).then_inc(h_hi, 1)
                    if sides:
                        sides(2 + mt)

            def gate_or_beside(u, s):
                if (u, s) == (EXP + 1, 1):
                    gate_exp(1)
                beside_experts(stages, u, s)

            for u in range(EXP + 2):
                unit(u // 2, u % 2, lambda s: gate_or_beside(u, s))
            with act.Fori(5, 7) as t:
                for k in range(2):
                    unit(t, k)
            unit(7, 0)
            unit(7, 1)

        @block.vector
        def _(dve):
            sub, mult, add = ALU.subtract, ALU.mult, ALU.add

            def stats(a, k, b):
                need(dve, ln_mv[a], k)
                for i in range(2):
                    s = dve.bn_stats(st[a][:, i, :], x[:, b + i, :])
                s.then_inc(ln_st[a], 1)
                dve.wait_ge(ln_st[a], k + 1)
                need(dve, ln_x[a], k)
                for i in range(2):
                    s = dve.bn_aggr(mv[a][:, i, :], st[a][:, i, :])
                s.then_inc(ln_mv[a], 1)
                dve.wait_ge(ln_mv[a], k + 1)
                need(dve, ln_rs[a], k)
                dve.tensor_scalar(veps[a][:], mv[a][:, :, 1], EPS, None, add).then_inc(ln_ve[a], 1)

            def normalised(a, k, b):
                need(dve, ln_rs[a], k + 1)
                need(dve, x3_psum if a else ln_T, k)
                for i in range(2):
                    s = dve.tensor_scalar(lnx[a][:, i, :], x[:, b + i, :], mv[a][:, i, 0:1],
                                          rstd[a][:, i:i + 1], sub, mult)
                s.then_inc(ln_x[a], 1)

            def ln1_lo(pr, h, hp_):
                need(dve, xn_hi, pr + 1)
                c = slice(2 * S * hp_, 2 * S * (hp_ + 1))
                dve.tensor_tensor(xnT[h][1][:, :, c], aux[:].rearrange("p (k t) -> p k t", k=KT),
                                  xnT[h][0][:, :, c].bitcast(F32), sub).then_inc(xn_lo, 1)

            def lo_w(p, i):
                if live(p, NH // 2 + 1):
                    need(dve, w_hi, p)
                    dve.tensor_tensor(w_s[i][1][:], w_st[i][:], w_s[i][0][:].bitcast(F32), sub).then_inc(w_lo, 1)

            def lo_wo(p, i):
                need(dve, wo_hi, p + 1)
                dve.tensor_tensor(wo_s[i][1][:], wo_st[i][:], wo_s[i][0][:].bitcast(F32), sub).then_inc(wo_lo, 1)

            def add_out(w, j, half):
                need(dve, wo_psum, w + 1)
                if isinstance(w, int):
                    half = w // NH
                    if NH <= w < NH + 2:
                        dve.wait_ge(x_bo, w - NH + 3)
                need(dve, wo_add, w)
                b = HALF * half + 2 * (j % 2)
                xb = x[:, b:b + 2, :]
                dve.tensor_tensor(xb, w_ps[:].rearrange("p (b d) -> p b d", b=2), xb, add).then_inc(wo_add, 1)

            def softmax_max(n):
                need(dve, s_psum, n + 1)
                need(dve, n_max, n)
                dve.tensor_reduce(mx[:], s_ps[:].rearrange("p (b k) -> p b k", b=HALF), AX.X,
                                  ALU.max).then_inc(s_max, 1)
                dve.wait_ge(s_max, n + 1)
                need(dve, e_done, n)
                dve.tensor_scalar(nmx[:], mx[:], -SCALE, None, mult).then_inc(n_max, 1)

            def softmax_norm(n):
                need(dve, e_done, n + 1)
                need(dve, p_norm, n)
                dve.reciprocal(rinv[:], rsum[:]).then_inc(r_inv, 1)
                dve.wait_ge(r_inv, n + 1)
                need(dve, t_psum, n)
                ri = rinv[:].rearrange("p (b o) -> p b o", o=1).broadcast_to([P, HALF, S])
                dve.tensor_tensor(pn[:], e_sb[:], ri, mult).then_inc(p_norm, 1)

            def gated(u, mt):
                r = 2 * u + mt
                need(dve, sl_s, r + 1)
                need(dve, hg_psum, r + 1)
                need(dve, h_lo[mt], u)
                dve.tensor_tensor(hp[:, mt, :], sl[:, mt, :], hg_ps[mt][:], mult).then_inc(h_s, 1)

            def lo_of(n, ps, hi, lo, bias, ready, done):
                need(dve, ready, n + 1)
                dve.scalar_tensor_tensor(lo, ps[:], bias, hi.bitcast(F32), add, sub).then_inc(done, 1)

            def maxima(pr):
                need(dve, uk_cp, pr + 1)
                if pr == 0:
                    dve.wait_ge(pads, 1)
                dve.tensor_tensor_scan(flat(pp), flat(decay), flat(kp[pr % 2]), 0.0, add, ALU.max).then_inc(p_scan, 1)
                dve.wait_ge(p_scan, pr + 1)
                need(dve, n1_s, pr)
                dve.tensor_tensor(seg(ap), before(pp), uk[pr][:], ALU.max).then_inc(q_max, 1)
                dve.wait_ge(q_max, pr + 1)
                need(dve, e12_exp, pr)
                dve.tensor_tensor(seg(dd, 0), before(pp), seg(ap), sub)
                dve.tensor_tensor(seg(dd, 1), uk[pr][:], seg(ap), sub).then_inc(d12_sub, 1)

            def scans(pr):
                if pr == 0:
                    dve.wait_ge(ctx_in_s, 16)
                need(dve, e34_exp, pr + 1)
                for ct in range(KT):
                    v = ctxT[:, ct, 2 * pr * S:2 * (pr + 1) * S].rearrange("p (b t) -> p b t", b=2)
                    i = dve.tensor_tensor(vp[:, 2 * ct:2 * ct + 2, 1:SEG],
                                          ee[:, 6 * KT + 2 * ct:6 * KT + 2 * ct + 2, 1:SEG], v, mult)
                i.then_inc(v_mul, 1)
                need(dve, v_mul, pr + 1)
                dve.tensor_tensor_scan(flat(ap), flat(ee, 2), flat(vp), 0.0, mult, add).then_inc(a_scan, 1)
                dve.tensor_tensor_scan(flat(bp), flat(ee, 2), flat(ee, 3), 0.0, mult, add).then_inc(b_scan, 1)

            def sums(pr):
                need(dve, n1_s, pr + 1)
                need(dve, n2_s, pr + 1)
                dve.tensor_tensor(num[:], num[:], uk[pr][:], add).then_inc(num_s, 1)
                need(dve, d1_s, pr + 1)
                dve.tensor_tensor(den[:], den[:], seg(ee, 1), add).then_inc(den_s, 1)

            def inverse_1(pr):
                dve.wait_ge(den_s, pr + 1)
                dve.reciprocal(tq[:, 0:2, :], den[:, 0:2, :]).then_inc(rec_s, 1)

            def inverse_2(pr):
                dve.reciprocal(tq[:, 2:4, :], den[:, 2:4, :]).then_inc(rec_s, 1)
                dve.wait_ge(rec_s, 2 * pr + 2)
                dve.tensor_tensor(num[:], num[:], tq[:], mult).then_inc(y_s, 1)

            def add_y(pr):
                b = 2 * pr
                need(dve, y_psum, pr + 1)
                for i in range(2):
                    s = dve.tensor_tensor(x[:, b + i, :], b_bank(pr)[:, D * i:D * (i + 1)], x[:, b + i, :], add)
                s.then_inc(x2_s, 1)
                dve.wait_ge(x2_s, pr + 1)
                stats(1, pr, b)

            def logits(pr):
                b = 2 * pr
                need(dve, lg_psum, pr + 1)
                for i in range(2):
                    s = dve.tensor_tensor(lg[:, b + i, :], b_bank(pr)[:, NE * i:NE * (i + 1)], row[:, R_GB:R_GB + NE],
                                          add)
                s.then_inc(lg_s, 1)

            def first_mul_of(mat):
                dve.wait_ge(first_in[mat], 32)
                w0 = matrix(w_st[0], mat)
                dve.tensor_tensor(w0, w0, matrix(s_st[0], mat), mult).then_inc(first_mul[mat], 1)

            def first_lo_of(mat):
                dve.wait_ge(first_hi[mat], 1)
                dve.tensor_tensor(matrix(w_s[0][1], mat), matrix(w_st[0], mat),
                                  matrix(w_s[0][0], mat).bitcast(F32), sub).then_inc(first_lo[mat], 1)

            dve.wait_ge(x_in_s[0], 16)
            stats(0, 0, 0)
            first_mul_of(0)
            normalised(0, 0, 0)
            dve.wait_ge(x_in_s[1], 16)
            stats(0, 1, 2)
            first_lo_of(0)
            first_mul_of(1)
            normalised(0, 1, 2)
            ln1_lo(0, 0, 0)
            first_lo_of(1)
            ln1_lo(1, 0, 1)
            dve.wait_ge(cst_in, 16)

            def recurrence_constants():
                for t, v in ((kp[0], EMPTY), (kp[1], EMPTY), (vp, 0.0), (ee, 0.0)):
                    dve.memset(t[:, :, 0], v).then_inc(consts_done, 1)
                dve.memset(we[:], 1.0).then_inc(consts_done, 1)
                dve.memset(decay[:], 0.0).then_inc(consts_done, 1)
                dve.wait_ge(wneg_s, 1)
                dve.tensor_scalar(wneg[:], wneg[:], -1.0, None, mult).then_inc(dec_s, 1)
                dve.wait_ge(dec_s, 1)
                dve.wait_ge(consts_done, 6)
                for ct in range(KT):
                    c = decay[:, 2 * ct:2 * ct + 2, 1:SEG]
                    dve.tensor_scalar(c, c, wneg[:, ct:ct + 1], None, add)
                dve.memset(decay[:, :, 0], RESET).then_inc(pads, 1)

            def step(it, j, half, sides=None):
                m = 4 * it + j
                head = lambda i: i % NH if isinstance(i, int) else i - NH * half
                if live(m - 1, STEPS):
                    softmax_max(m - 1)
                if live(m - 4, STEPS):
                    add_out(m - 4, j, half)
                if live(m - 1, STEPS):
                    softmax_norm(m - 1)
                if isinstance(m, int) and m == STEPS + 1:
                    for mt in range(2):
                        gated(0, mt)
                if sides:
                    sides(m, 0)
                if live(m - 2, STEPS):
                    n, i = m - 2, (j - 2) % 4
                    lo_of(n, o_ps, o_s[0][:, i, :], o_s[1][:, i, :], cst[:, bass.ds(C_BV + head(n), 1)],
                          o_hi, o_lo)
                if live(m, STEPS):
                    need(dve, k_psum, m + 1)
                    dve.tensor_scalar(k_sb[:], k_ps[:], cst[:, bass.ds(C_BK + head(m), 1)], None,
                                      add).then_inc(k_done, 1)
                    if isinstance(m, int) and m < 2:
                        if m == 1:
                            lo_w(1, 1)
                    elif j % 2 == 0:
                        lo_w(2 * it + 1 + j // 2, (1 + j // 2) % 2)
                    if j % 2:
                        lo_wo(2 * it + j // 2, j // 2)
                if sides:
                    sides(m, 1)

            def first_norms(j, s):
                if (j, s) == (0, 1):
                    dve.wait_ge(x_in_s[2], 16)
                    stats(0, 2, HALF)
                elif s == 0 and j >= 2:
                    normalised(0, j, HALF + 2 * (j - 2))
                elif s == 1 and j >= 2:
                    if j == 2:
                        stats(0, 3, HALF + 2)
                    ln1_lo(j, 1, j - 2)

            def stats_a(pr):
                dve.wait_ge(wo_add, NH * (pr // 2 + 1) - 1 + pr % 2)
                stats(0, 4 + pr, 2 * pr)

            stages = {
                "stats_a": stats_a, "norm_a": lambda pr: normalised(0, 4 + pr, 2 * pr), "maxima": maxima,
                "scans": scans, "sums": sums, "inverse_1": inverse_1, "inverse_2": inverse_2, "add_y": add_y,
                "norm_b": lambda pr: normalised(1, pr, 2 * pr), "logits": logits,
            }
            for j in range(4):
                step(0, j, 0, first_norms)
            dve.wait_ge(x_bo, 2)
            with dve.Fori(1, 4) as it:
                for j in range(4):
                    step(it, j, 0)
            def gate(h, part):
                c = slice(HALF * h, HALF * (h + 1))
                cast = lambda t: t.rearrange("p (b o) -> p b o", o=1).broadcast_to([P, HALF, NE])
                count = [GATE_STEPS * h + sum(GATE_PARTS[:part])]

                def then(i):
                    count[0] += 1
                    i.then_inc(g_step, 1)
                    dve.wait_ge(g_step, count[0])

                if part == 0:
                    dve.wait_ge(lg_s, 2 * (h + 1))
                    then(dve.tensor_reduce(gs[:], lg[:, c, :], AX.X, ALU.max))
                    then(dve.tensor_tensor(g1[:], lg[:, c, :], cast(gs[:]), sub))
                elif part == 1:
                    dve.wait_ge(g_exp, h + 1)
                    then(dve.tensor_reduce(gs[:], gp[:], AX.X, add))
                    then(dve.reciprocal(gr[:], gs[:]))
                    then(dve.tensor_tensor(g2[:], gp[:], cast(gr[:]), mult))
                    bias = row[:, R_BIAS:R_BIAS + NE].rearrange("p (o e) -> p o e", o=1).broadcast_to([P, HALF, NE])
                    then(dve.tensor_tensor(gb[:], g2[:], bias, add))
                    other = gb[:].rearrange("p b (o j) -> p b o j", o=1).broadcast_to([P, HALF, NE, NE])
                    own = gb[:].rearrange("p b (e o) -> p b e o", o=1).broadcast_to([P, HALF, NE, NE])
                    before_ = tri[:].rearrange("p (o e) j -> p o e j", o=1).broadcast_to([P, HALF, NE, NE])
                    then(dve.tensor_tensor(r1[:], other, own, ALU.is_gt))
                    then(dve.tensor_tensor(r2[:], other, own, ALU.is_equal))
                    then(dve.tensor_tensor(r2[:], r2[:], before_, mult))
                else:
                    then(dve.tensor_tensor(r1[:], r1[:], r2[:], add))
                    then(dve.tensor_reduce(g1[:], r1[:], AX.X, add))
                    then(dve.scalar_tensor_tensor(g1[:], g1[:], float(TOPK), g2[:], ALU.is_lt, mult))
                    then(dve.tensor_reduce(gs[:], g1[:], AX.X, add))
                    then(dve.reciprocal(gr[:], gs[:]))
                    dve.wait_ge(consts_done, 6)
                    then(dve.tensor_tensor(we[:, c, 0:NE], g1[:], cast(gr[:]), mult))

            def lo_h(u, k=0):
                need(dve, h_hi, 2 * u + 1)
                dve.tensor_tensor(o_s[1][:, 2 * k, :], hp[:, 0, :], o_s[0][:, 2 * k, :].bitcast(F32),
                                  sub).then_inc(h_lo[0], 1)

            for m in range(NH, STEPS + 4):
                step(m // 4, m % 4, 1, lambda m, s: beside_attention(stages, m, s))
                if m == NH:
                    recurrence_constants()
                elif m == STEPS:
                    gate(0, 0)
                elif m == STEPS + 1:
                    gate(0, 1)
                elif m == STEPS + 2:
                    lo_h(0)
                    gate(0, 2)

            def add_expert(u, half):
                for bb in range(2):
                    need(dve, y2_psum, 2 * u + bb + 1)
                    need(dve, acc, 2 * u + bb - 1)
                    for i in range(2):
                        b = HALF * half + 2 * bb + i
                        e = u - EXP * half
                        s = dve.scalar_tensor_tensor(x[:, b, :], y_ps[bb][:, D * i:D * (i + 1)],
                                                     we[:, b, bass.ds(e, 1)], x[:, b, :], mult, add)
                    s.then_inc(acc, 1)

            def unit(t, k, half, sides=None):
                u = 2 * t + k
                if not (isinstance(u, int) and u < 2):
                    lo_h(u - 1, (k + 1) % 2)
                if sides:
                    sides(u, 0)
                if live(u - 2, UNITS):
                    add_expert(u - 2, (u - 2) // EXP if isinstance(u, int) else half)
                if sides:
                    sides(u, 1)
                for mt in range(2):
                    if not (isinstance(u, int) and u == 0):
                        gated(u, mt)
                    if sides:
                        sides(u, 2 + mt)

            def gate_or_beside(u, s):
                beside_experts(stages, u, s)
                if (u, s) == (EXP + 1, 0):
                    gate(1, 0)
                elif u == EXP + 1 and s >= 2:
                    gate(1, s - 1)

            for u in range(EXP + 2):
                unit(u // 2, u % 2, u // EXP, gate_or_beside)
            with dve.Fori(5, 7) as t:
                for k in range(2):
                    unit(t, k, 1)
            unit(7, 0, 1)
            unit(7, 1, 1)
            lo_h(15, 1)
            add_expert(14, 1)
            add_expert(15, 1)

        @block.tensor
        def _(pe):
            def split_mm(out_, pairs):
                every = [(l[a], r[b]) for l, r in pairs for a, b in PASSES]
                for i, (l, r) in enumerate(every):
                    mm = pe.matmul(out_, l, r, start=i == 0, stop=i == len(every) - 1)
                return mm

            def ln_transpose(a, k, bank_):
                need(pe, ln_x[a], k + 1)
                for kt in range(KT):
                    for b in range(2):
                        at = (2 * kt + b) * S
                        mm = pe.transpose(bank_[:, at:at + S], lnx[a][:, b, kt * P:(kt + 1) * P], ident[:])
                return mm

            def ln1_T(pr):
                need(pe, xn_lo, pr)
                ln_transpose(0, pr, aux).then_inc(ln_T, 1)

            def scores(n):
                need(pe, q_done, n + 1)
                need(pe, k_done, n + 1)
                need(pe, e_done, n)
                for b in range(HALF):
                    c = slice(b * S, (b + 1) * S)
                    mm = pe.matmul(s_ps[:, c], q_sb[:, c], k_sb[:, c], start=True, stop=True)
                mm.then_inc(s_psum, 1)

            def attend(n, j, vcount):
                need(pe, pt_cp, n + 1)
                need(pe, v_cp, vcount)
                need(pe, o_lo, n)
                i, f = j // 2, (j % 2) * DH
                for b in range(HALF):
                    mm = pe.matmul(o_ps[:, b * S:(b + 1) * S], v_sb[i][:, b, f:f + DH], pT[:, b, :],
                                   start=True, stop=True)
                mm.then_inc(o_psum, 1)

            def project(m, j, half, pair):
                i, f = j // 2, (j % 2) * DH
                xs = xnT[half]
                if not (isinstance(pair, int) and pair == 0):
                    need(pe, w_lo, pair)
                need(pe, xn_lo, 2 * (half + 1))
                for mat, ps, ready, used in ((0, q_ps, q_psum, q_done), (1, k_ps, k_psum, k_done)):
                    if isinstance(m, int) and m == 0:
                        pe.wait_ge(first_lo[mat], 1)
                    need(pe, used, m)
                    split_mm(ps[:], [([qkv(i, s, kt, mat, f, f + DH) for s in range(2)],
                                      [xs[s][:, kt, :] for s in range(2)]) for kt in range(KT)]).then_inc(ready, 1)
                need(pe, v_cp, m)
                if isinstance(m, int) and m == 0:
                    pe.wait_ge(first_lo[2], 1)
                for b in range(2):
                    t = (2 * (j % 2) + b) * S
                    mm = split_mm(v_ps[:, 2 * DH * b:2 * DH * (b + 1)],
                                  [([xs[s][:, kt, t:t + S] for s in range(2)],
                                    [qkv(i, s, kt, 2, 0, 2 * DH) for s in range(2)]) for kt in range(KT)])
                mm.then_inc(v_psum, 1)

            def prob_T(n):
                need(pe, p_norm, n + 1)
                need(pe, pt_cp, n)
                for b in range(HALF):
                    mm = pe.transpose(t_ps[:, b * S:(b + 1) * S], pn[:, b, :], ident[:])
                mm.then_inc(t_psum, 1)

            def project_out(w, j, pair):
                need(pe, o_lo, 2 * pair + 2)
                need(pe, wo_lo, pair + 1)
                need(pe, wo_add, w)
                i = j // 2
                for b in range(2):
                    t = (2 * (j % 2) + b) * S
                    mm = split_mm(w_ps[:, D * b:D * (b + 1)],
                                  [([o_s[s][:, 2 * i + h, t:t + S] for s in range(2)],
                                    [wo_s[i][s][:, D * h:D * (h + 1)] for s in range(2)]) for h in range(2)])
                mm.then_inc(wo_psum, 1)

            def step(it, j, half, sides=None):
                m = 4 * it + j
                if live(m - 1, STEPS):
                    scores(m - 1)
                if live(m - 2, STEPS):
                    attend(m - 2, (j - 2) % 4, 4 * it + 2 * ((j - 2) // 2) + 2)
                if live(m, STEPS):
                    project(m, j, half, 2 * it + j // 2)
                if sides:
                    sides(m, 0)
                if live(m - 1, STEPS):
                    prob_T(m - 1)
                if live(m - 3, STEPS):
                    project_out(m - 3, (j - 3) % 4, 2 * it + (j - 3) // 2)
                if sides:
                    sides(m, 1)

            def first_norms(j, s):
                if s == 0 and j >= 2:
                    ln1_T(j)

            def keys_T(pr):
                need(pe, xn_lo, 4)
                need(pe, k_cp, pr)
                if pr == 2:
                    pe.wait_ge(lg_s, 2)
                ln_transpose(0, 4 + pr, aux).then_inc(ln_T, 1)

            def outputs_T(pr):
                need(pe, y_s, pr + 1)
                bank_ = b_bank(pr)
                if pr == 0:
                    pe.wait_ge(k_cp, 2)
                elif pr == 2:
                    pe.wait_ge(pt_cp, STEPS)
                else:
                    pe.wait_ge(lg_s, pr)
                for b in range(2):
                    for ct in range(KT):
                        at = D * b + P * ct
                        mm = pe.transpose(bank_[:, at:at + P], num[:, 2 * ct + b, :], ident[:])
                mm.then_inc(y_psum, 1)

            def x3_T(pr):
                need(pe, x2_s, pr + 1)
                ln_transpose(1, pr, b_bank(pr)).then_inc(x3_psum, 1)

            def gate_logits(pr):
                need(pe, x3_cp, pr + 1)
                if pr == 0:
                    pe.wait_ge(cst_in, 16)
                for b in range(2):
                    for kt in range(KT):
                        at = C_GATE + NE * kt
                        mm = pe.matmul(b_bank(pr)[:, NE * b:NE * (b + 1)], x3f[:, kt, b * S:(b + 1) * S],
                                       cst[:, at:at + NE], start=kt == 0, stop=kt == KT - 1)
                mm.then_inc(lg_psum, 1)

            stages = {"keys_T": keys_T, "outputs_T": outputs_T, "x3_T": x3_T, "gate_logits": gate_logits}
            pe.wait_ge(idn, 5)
            ln1_T(0)
            ln1_T(1)
            for j in range(4):
                step(0, j, 0, first_norms)
            with pe.Fori(1, 4) as it:
                for j in range(4):
                    step(it, j, 0)

            def up_projection(u, k, half, mt):
                need(pe, w_lo, NH + u)
                need(pe, x3_lo, 2 * (half + 1))
                xs = x3T[half]
                if isinstance(u, int) and u == 0:
                    for used in ((q_done, k_done), (v_cp, e_done))[mt]:
                        pe.wait_ge(used, STEPS)
                for mat, ps, ready, used in ((0, h1_ps, h1_psum, sl_s), (1, hg_ps, hg_psum, h_s)):
                    need(pe, used, 2 * u + mt - 1)
                    split_mm(ps[mt][:], [([up(k, s, kt, mat, mt) for s in range(2)],
                                          [xs[s][:, kt, :] for s in range(2)])
                                         for kt in range(KT)]).then_inc(ready, 1)

            def down_projection(u, k, bb):
                for lo in h_lo:
                    need(pe, lo, u + 1)
                need(pe, wo_lo, NH + u + 1)
                if isinstance(u, int) and u == 0:
                    pe.wait_ge((o_lo, wo_add)[bb], STEPS)
                need(pe, acc, 2 * u + bb - 1)
                for i in range(2):
                    t = (2 * bb + i) * S
                    mm = split_mm(y_ps[bb][:, D * i:D * (i + 1)],
                                  [([o_s[s][:, 2 * k + kt, t:t + S] for s in range(2)],
                                    [wo_s[k][s][:, D * kt:D * (kt + 1)] for s in range(2)])
                                   for kt in range(KT)])
                mm.then_inc(y2_psum, 1)

            def end_or_beside(m, s):
                if STEPS <= m < STEPS + 2:
                    up_projection(m - STEPS, m - STEPS, 0, s)
                else:
                    beside_attention(stages, m, s)

            for m in range(NH, STEPS + 3):
                step(m // 4, m % 4, 1, end_or_beside)
            for s in range(6):
                beside_experts(stages, s // 4, s % 4)
            for u in range(1, EXP + 2):
                for i in range(4):
                    if u == 1 and i < 2:
                        continue
                    if i < 2:
                        up_projection(u, u % 2, u // EXP, i)
                    else:
                        down_projection(u - 1, (u - 1) % 2, i - 2)
                    beside_experts(stages, u, i)
            with pe.Fori(5, 8) as t:
                for k in range(2):
                    u = 2 * t + k
                    for mt in range(2):
                        up_projection(u, k, 1, mt)
                    for bb in range(2):
                        down_projection(u - 1, (k + 1) % 2, bb)
            for bb in range(2):
                down_projection(15, 1, bb)


def kernel(**inputs):
    import numpy as np
    import concourse.bacc as bacc
    from concourse import mybir as mb
    from concourse.bass_utils import run_bass_kernel_spmd

    a = {k: np.asarray(v) for k, v in inputs.items()}
    pairs = NH // 2

    def by_pair(mats, rows, tiles):
        t = np.stack(mats).reshape(len(mats), tiles, rows, pairs, 2 * DH)
        return np.ascontiguousarray(t.transpose(3, 2, 0, 1, 4)).reshape(pairs, rows, -1)

    def over_block(s):
        return s

    wqkv = by_pair([a[f"L0_attn_w{c}_codes"] for c in "qkv"], P, KT)
    sqkv = by_pair([a[f"L0_attn_w{c}_scales"] for c in "qkv"], P // BLK, KT)
    wo = a["L0_attn_wo_codes"].reshape(pairs, 2, P, D).transpose(0, 2, 1, 3).reshape(pairs, P, OW)
    so = a["L0_attn_wo_scales"].reshape(pairs, 2, P // BLK, D).transpose(0, 2, 1, 3).reshape(pairs, P // BLK, OW)
    w1 = np.concatenate([a["L0_ffn_W1"], a["L0_ffn_Ws1"][None]])
    wg = np.concatenate([a["L0_ffn_Wg"], a["L0_ffn_Wsg"][None]])
    w2 = np.concatenate([a["L0_ffn_W2"], a["L0_ffn_Ws2"][None]])
    wup = np.stack([w1, wg], 1).reshape(EXP, 2, KT, P, D).transpose(0, 3, 2, 1, 4).reshape(EXP, P, HW)
    wdown = w2.reshape(EXP, KT, P, D).transpose(0, 2, 1, 3).reshape(EXP, P, OW)
    cols = [a[f"L0_attn_b{c}"].reshape(NH, DH).T for c in "qkv"]
    cols += [a[f"L0_xattn_time_{c}"].reshape(KT, P).T for c in ("decay", "first")]
    cols += [a["L0_ffn_gate_w"].reshape(KT, P, NE).transpose(1, 0, 2).reshape(P, KT * NE)]
    rows = np.concatenate([a["L0_attn_bo"], a["L0_ffn_gate_b"], a["L0_ffn_biases"]])[None]
    arrays = {
        "x_in": a["x"].transpose(1, 0, 2),
        "ctx_in": a["ctx_2048"].reshape(NB * S, KT, P).transpose(2, 1, 0),
        "wqkv": wqkv, "sqkv": sqkv, "wo": wo, "so": so, "wup": wup, "wdown": wdown,
        "consts": np.concatenate(cols, 1), "rows": rows,
    }
    arrays = {k: np.ascontiguousarray(v) for k, v in arrays.items()}
    nc = bacc.Bacc("TRN2", target_bir_lowering=False, num_devices=1)
    t = {k: nc.dram_tensor(k, v.shape, mb.dt.from_np(v.dtype), kind="ExternalInput").ap()
         for k, v in arrays.items()}
    out = nc.dram_tensor("out", (S, NB, D), mb.dt.from_np(arrays["x_in"].dtype), kind="ExternalOutput").ap()
    decoder_layer(nc, t["x_in"], t["ctx_in"], t["wqkv"], t["sqkv"], t["wo"], t["so"], t["wup"], t["wdown"],
                  t["consts"], t["rows"], out)
    r = run_bass_kernel_spmd(nc, [arrays], core_ids=[0])
    return np.ascontiguousarray(r.results[0]["out"].transpose(1, 0, 2))
```
